# Optimizing a Trainium2 kernel written in Bass

```python
import numpy as np
import jax
import jax.numpy as jnp

def _softmax(x, axis=-1):
    return jax.nn.softmax(x, axis=axis)

def _gelu(x):
    return jax.nn.gelu(x, approximate=True)

def _silu(x):
    return jax.nn.silu(x)

def _sigmoid(x):
    return jax.nn.sigmoid(x)

def _layernorm(x, axis=-1, eps=1e-05):
    m = jnp.mean(x, axis=axis, keepdims=True)
    v = jnp.var(x, axis=axis, keepdims=True)
    return (x - m) / jnp.sqrt(v + eps)

def _scatter_add(tgt, idx, src, axis=0):
    return tgt.at[idx].add(src)

def _segment_sum(src, seg, n):
    return jax.ops.segment_sum(src, seg, n)
kernel_name = 'mk_adaln_d1_jaxref_r4_d05638'

def setup_inputs(seed: int=0):
    np.random.seed(seed)
    _w = jnp.asarray

    def _L0_attn_setup():
        import jax, jax.numpy as jnp
        import numpy as np
        import math
        N_HEAD = 16
        EPS = 1e-06

        def _phi(x, omega):
            m = omega.shape[1]
            proj = jnp.einsum('bhtd,dm->bhtm', x, omega)
            norm_sq_half = 0.5 * jnp.sum(x * x, axis=-1, keepdims=True)
            return jnp.exp(proj - norm_sq_half) / math.sqrt(m)
        key = jax.random.key(seed)
        ks = jax.random.split(key, 4)
        B, T, C = (2, 256, 256)
        d_h, m = (C // N_HEAD, 128)
        x = jax.random.normal(ks[0], (B, T, C), dtype=jnp.float32)
        W_attn = jax.random.normal(ks[1], (C, 3 * C), dtype=jnp.float32) * (1.0 / math.sqrt(C))
        b_attn = jnp.zeros((3 * C,), dtype=jnp.float32)
        W_proj = jax.random.normal(ks[2], (C, C), dtype=jnp.float32) * (1.0 / math.sqrt(C))
        b_proj = jnp.zeros((C,), dtype=jnp.float32)
        omega = jax.random.normal(ks[3], (d_h, m), dtype=jnp.float32)
        return {'x': x, 'W_attn': W_attn, 'b_attn': b_attn, 'W_proj': W_proj, 'b_proj': b_proj, 'omega': omega}
    _L0_attn_in = _L0_attn_setup()

    def _L0_ffn_setup():
        import jax, jax.numpy as jnp
        import numpy as np
        TOP_K = 2
        key = jax.random.key(seed)
        ks = jax.random.split(key, 7)
        B_, S, D, F, E, R = (2, 512, 256, 1024, 4, 4)
        x = jax.random.normal(ks[0], (B_, S, D), dtype=jnp.float32)
        Wg = jax.random.normal(ks[1], (E, D), dtype=jnp.float32) * (1.0 / np.sqrt(D))
        bg = jnp.zeros((E,), dtype=jnp.float32)
        Wi = jax.random.normal(ks[2], (F, D), dtype=jnp.float32) * (1.0 / np.sqrt(D))
        Wo = jax.random.normal(ks[3], (D, F), dtype=jnp.float32) * (1.0 / np.sqrt(F))
        A = jax.random.normal(ks[4], (E, R, D), dtype=jnp.float32) * (1.0 / np.sqrt(D))
        Bm = jax.random.normal(ks[5], (E, F, R), dtype=jnp.float32) * 0.01
        return {'x': x, 'Wg': Wg, 'bg': bg, 'Wi': Wi, 'Wo': Wo, 'A': A, 'B': Bm}
    _L0_ffn_in = _L0_ffn_setup()
    _L0_c = _w((lambda *s: np.random.randn(*s).astype(np.float32) * 0.05)(2, 256))
    _L0_wmod = _w((lambda *s: np.random.randn(*s).astype(np.float32) * 0.05)(256, 6 * 256) * 256 ** (-0.5))
    _d = {'L0_attn_x': _L0_attn_in['x'], 'L0_attn_W_attn': _L0_attn_in['W_attn'], 'L0_attn_b_attn': _L0_attn_in['b_attn'], 'L0_attn_W_proj': _L0_attn_in['W_proj'], 'L0_attn_b_proj': _L0_attn_in['b_proj'], 'L0_attn_omega': _L0_attn_in['omega'], 'L0_ffn_Wg': _L0_ffn_in['Wg'], 'L0_ffn_bg': _L0_ffn_in['bg'], 'L0_ffn_Wi': _L0_ffn_in['Wi'], 'L0_ffn_Wo': _L0_ffn_in['Wo'], 'L0_ffn_A': _L0_ffn_in['A'], 'L0_ffn_B': _L0_ffn_in['B'], 'L0_c': _L0_c, 'L0_wmod': _L0_wmod}
    _x0 = _d['L0_attn_x']
    _d['L0_attn_x'] = jax.random.normal(jax.random.fold_in(jax.random.key(seed), 1), (2, 2048, 256), dtype=_x0.dtype)
    del _x0
    return _d

def reference(L0_attn_x, L0_attn_W_attn, L0_attn_b_attn, L0_attn_W_proj, L0_attn_b_proj, L0_attn_omega, L0_ffn_Wg, L0_ffn_bg, L0_ffn_Wi, L0_ffn_Wo, L0_ffn_A, L0_ffn_B, L0_c, L0_wmod):

    def _L0_attn_ref(x, W_attn, b_attn, W_proj, b_proj, omega):
        import jax, jax.numpy as jnp
        import numpy as np
        import math
        N_HEAD = 16
        EPS = 1e-06

        def _phi(x, omega):
            m = omega.shape[1]
            proj = jnp.einsum('bhtd,dm->bhtm', x, omega)
            norm_sq_half = 0.5 * jnp.sum(x * x, axis=-1, keepdims=True)
            return jnp.exp(proj - norm_sq_half) / math.sqrt(m)
        B, T, C = x.shape
        nh = N_HEAD
        d_h = C // nh
        qkv = x @ W_attn + b_attn
        q, k, v = jnp.split(qkv, 3, axis=-1)
        q = q.reshape(B, T, nh, d_h).transpose(0, 2, 1, 3)
        k = k.reshape(B, T, nh, d_h).transpose(0, 2, 1, 3)
        v = v.reshape(B, T, nh, d_h).transpose(0, 2, 1, 3)
        scale = 1.0 / math.sqrt(d_h)
        q = q * scale
        k = k * scale
        phi_q = _phi(q, omega)
        phi_k = _phi(k, omega)
        kv = phi_k[..., :, None] * v[..., None, :]
        S = jnp.cumsum(kv, axis=2)
        Z = jnp.cumsum(phi_k, axis=2)
        num = jnp.einsum('bhtm,bhtmd->bhtd', phi_q, S)
        den = jnp.einsum('bhtm,bhtm->bht', phi_q, Z)[..., None] + EPS
        y = num / den
        y = y.transpose(0, 2, 1, 3).reshape(B, T, C)
        return y @ W_proj + b_proj

    def _L0_ffn_ref(x, Wg, bg, Wi, Wo, A, B):
        import jax, jax.numpy as jnp
        import numpy as np
        TOP_K = 2
        E = Wg.shape[0]
        logits = jnp.einsum('bsd,ed->bse', x, Wg) + bg
        scores = jax.nn.softmax(logits, axis=-1)
        topv, topi = jax.lax.top_k(scores, TOP_K)
        w = jnp.sum(jax.nn.one_hot(topi, E, dtype=x.dtype) * topv[..., None], axis=-2)
        base = jnp.einsum('bsd,fd->bsf', x, Wi)
        lora_low = jnp.einsum('bsd,erd->bser', x, A)
        lora = jnp.einsum('bser,efr->bsef', lora_low, B)
        h = jax.nn.relu(base[:, :, None, :] + lora)
        expert_out = jnp.einsum('bsef,df->bsed', h, Wo)
        out = jnp.einsum('bse,bsed->bsd', w, expert_out)
        return out
    x = L0_attn_x
    mod = (_silu(L0_c) @ L0_wmod).reshape(L0_c.shape[0], 6, 1, -1)
    sa, ca, ga, sb, cb, gb = (mod[:, 0], mod[:, 1], mod[:, 2], mod[:, 3], mod[:, 4], mod[:, 5])
    ga = (2 * (ga >= 0) - 1) * jnp.maximum(jnp.abs(ga), 0.25)
    gb = (2 * (gb >= 0) - 1) * jnp.maximum(jnp.abs(gb), 0.25)
    h = _layernorm(x, axis=-1) * (1 + ca) + sa
    x = x + ga * _L0_attn_ref(h, L0_attn_W_attn, L0_attn_b_attn, L0_attn_W_proj, L0_attn_b_proj, L0_attn_omega)
    h = _layernorm(x, axis=-1) * (1 + cb) + sb
    x = x + gb * _L0_ffn_ref(h, L0_ffn_Wg, L0_ffn_bg, L0_ffn_Wi, L0_ffn_Wo, L0_ffn_A, L0_ffn_B)
    return x

_drawn_inputs = setup_inputs


def setup_inputs(seed=0):
    import zlib

    import numpy as np

    out = dict(_drawn_inputs(seed))
    spreads = {'L0_attn_b_attn': (0.0, 0.1), 'L0_attn_b_proj': (0.0, 0.1), 'L0_ffn_bg': (0.0, 0.1)}
    factors = {}
    for name, (base, spread) in spreads.items():
        noise = np.random.default_rng([zlib.crc32(name.encode()), seed]).standard_normal(out[name].shape)
        drawn = base * np.exp(spread * noise) if base else spread * noise
        out[name] = jnp.asarray(drawn.astype(out[name].dtype))
    for name, factor in factors.items():
        out[name] = (out[name] * factor).astype(out[name].dtype)
    return out
```

```python
from contextlib import ExitStack

import concourse.bass as bass
from concourse import mybir

P = 128
B, SEQ, C = 2, 2048, 256
H, DH, M = 16, 16, 128
F, E, R = 1024, 4, 4
T = 512
NT = T // P
KT = C // P
FT = F // P
NB = B * SEQ // T
BLOCKS_PER_ROW = SEQ // T
PAIRS = H // 2
GROUP = 4
GROUPS = H // GROUP
VA = P // GROUP
HEAD_ROWS = 3 * DH
XROWS = 2 * HEAD_ROWS + 4
LORA = E * R
LROWS = 96
LOGIT_ROW = 96
EPS_LN = 1e-5
EPS_DEN = 1e-6 * M
Q_SCALE = DH ** -0.5
TILES = 6
PAD = -3.0e38

ALU = mybir.AluOpType
ACT = mybir.ActivationFunctionType
AX = mybir.AxisListType
F32 = mybir.dt.float32
F32R = mybir.dt.float32r
BF16 = mybir.dt.bfloat16

CONSTS = {"ident": P, "causal": P, "headsum": VA, "prio": E}


class Signal:

    def __init__(self, sem, per):
        self.sem, self.per = sem, per

    def at(self, n, c):
        return n * self.per + c


def wait(eng, signal, n, c):
    eng.wait_ge(signal.sem, signal.at(n, c))


def build(nc, x, w_attn, b_attn, w_proj, b_proj, omega, wg, bg, wi, wo, lora_a, lora_b, cond, wmod,
          consts, norm_rows, out):
    ctx = ExitStack()
    with ctx:
        def sb(name, shape, dt=F32):
            return ctx.enter_context(nc.sbuf_tensor(name, shape, dt))

        def sig(name, per=0):
            return Signal(ctx.enter_context(nc.semaphore(name)), per)

        const = sb("const", [P, sum(CONSTS.values())])
        at, cols = 0, {}
        for name, width in CONSTS.items():
            cols[name] = const[:, at:at + width]
            at += width
        ident, causal, headsum, prio = (cols[name] for name in CONSTS)
        wa_r, wa_l = sb("wa_r", [P, KT, 3 * C], F32R), sb("wa_l", [P, KT, 3 * C], F32R)
        wi_r, wi_l = sb("wi_r", [P, KT, F], F32R), sb("wi_l", [P, KT, F], F32R)
        wo_t = sb("wo_t", [P, FT, C])
        wp = sb("wp", [P, KT, C])
        low_t = sb("low_t", [P, KT, P])
        lora_w = sb("lora_w", [LROWS, F], F32R)
        omega_x = sb("omega_x", [XROWS, 2 * M], F32R)
        om_f, om_r, om_l = sb("om_f", [DH, M]), sb("om_r", [DH, M], F32R), sb("om_l", [DH, M], F32R)
        nrow_f, nrow_r = sb("nrow_f", [4, 2 * M]), sb("nrow_r", [4, 2 * M], F32R)
        qk_bias = sb("qk_bias", [P, 4])
        v_bias = sb("v_bias", [P, C])
        bp_row = sb("bp_row", [P, C])
        bg_row = sb("bg_row", [P, E])
        neg_half, eps = sb("neg_half", [P, NT]), sb("eps", [P, NT])
        mod1 = sb("mod1", [P, B, 2 * KT])
        mod2 = sb("mod2", [P, B, 3 * C + 2 * KT])
        mod1_now = sb("mod1_now", [P, 2 * KT])
        mod2_now = sb("mod2_now", [P, 3 * C])
        mod2_cols = sb("mod2_cols", [P, 2 * KT])
        ga_now, gb_now, bpg_now = (mod2_now[:, k * C:(k + 1) * C] for k in range(3))
        cT, sT = sb("cT", [P, KT, B]), sb("sT", [P, KT, B])
        lora_raw = sb("lora_raw", [P, FT, E, R])

        tok = sb("tok", [P, NT, C])
        xr = sb("xr", [P, NT, C])
        stats, mv = sb("stats", [P, NT, 6]), sb("mv", [P, NT, 2])
        var_eps, rstd = sb("var_eps", [P, NT]), sb("rstd", [P, NT])
        h_r, h_l = sb("h_r", [P, KT, T], F32R), sb("h_l", [P, KT, T], F32R)
        qk_r, qk_l = sb("qk_r", [P, 2, T], F32R), sb("qk_l", [P, 2, T], F32R)
        norm_r, norm_l = sb("norm_r", [P, T], F32R), sb("norm_l", [P, T], F32R)
        xq = sb("xq", [XROWS, 2, PAIRS, T], F32R)
        v_ones = sb("v_ones", [P, NT, H, VA])

        phq = sb("phq", [P, 2, GROUP, T])
        phkT = sb("phkT", [P, 2, 2, T])
        am_phk = sb("am_phk", [P, 3, GROUP, T])
        am = am_phk[:, 0]
        prod_sb, oT_sb = sb("prod_sb", [P, NT, 2, P]), sb("oT_sb", [P, NT, P])
        s_sb = sb("s_sb", [P, NT, P])
        state = sb("state", [P, 2, GROUPS, P])
        den, rden = sb("den", [P, NT, GROUP]), sb("rden", [P, NT, GROUP])
        y = sb("y", [P, NT, C])

        tg = sb("tg", [P, 2, 2 * C])
        low = sb("low", [LROWS, T], F32R)
        low1, low2 = sb("low1", [LROWS, T], F32R), sb("low2", [LROWS, T], F32R)
        mk1, mk2 = sb("mk1", [P, NT, LROWS]), sb("mk2", [P, NT, LROWS])
        route = sb("route", [P, 8, NT, E])
        rmax = sb("rmax", [P, 4, NT])
        ex, exo = sb("ex", [P, NT, E + 1]), sb("exo", [P, NT, E + 1])
        wsum, w1 = sb("wsum", [P, NT]), sb("w1", [P, NT])

        qk_sq = phq[:, 0]
        g, rho = phq[:, 1, 0:3], phq[:, 1, 3]
        yT = phkT[:, 0]
        r2, lg = am[:, 0:2], am[:, 2]
        h_f, qk_f = am_phk[:, 1, 0:2], am_phk[:, 1, 2:4]

        flat = lambda ap: ap.rearrange("p a t -> p (a t)")
        wmod_raw = [flat(phq[:, k])[:, 0:6 * C] for k in range(KT)]
        wa_raw = [flat(phkT[:, k])[:, 0:3 * C] for k in range(KT)]
        wi_raw = [flat(am_phk[:, 2, 2 * k:2 * k + 2]) for k in range(2)]
        wo_raw = [flat(am[:, 2 * k:2 * k + 2]) for k in range(KT)]
        low_raw = tg[:, 1, 0:C]
        s_rep = tg[:].rearrange("p b n -> p (b n)")[:, 0:KT * B * P].rearrange("p (k b m) -> p k b m", k=KT, b=B)

        def bank(name):
            return ctx.enter_context(nc.psum_tensor(name, [P, 512], F32))

        ring = [bank(f"ring{i}") for i in range(4)]
        pa = [bank("pa0"), bank("pa1")]
        prod = ctx.enter_context(nc.psum_tensor("prod", [P, NT, 2, P], F32))
        pb = [prod[:, 2 * b:2 * b + 2].rearrange("p c k m -> p (c k m)") for b in range(2)]
        qk_bank = [pa[0], pa[1], ring[2], ring[3]]
        z_bank = [ring[2], ring[3], ring[0], ring[1]]

        ld_first, ld_late, ld_low = sig("ld_first"), sig("ld_late"), sig("ld_low")
        om_parts, om_moved = sig("om_parts"), sig("om_moved")
        set_vec, set_act, set_pe, set_pool = sig("set_vec"), sig("set_act"), sig("set_pe"), sig("set_pool")
        late_pe, late_vec, late_act = sig("late_pe"), sig("late_vec"), sig("late_act")
        x_loaded, tok_free = sig("x_loaded", 16), sig("tok_free", 1)
        ln1_vec, ln1_pool, hn_ready = sig("ln1_vec", 9), sig("ln1_pool", 2), sig("hn_ready", 4)
        hT_ps, hT_full, hT_parts = sig("hT_ps", 2), sig("hT_full", 2), sig("hT_parts", 4)
        qk_ps, qk_full, sq_ready = sig("qk_ps", 4), sig("qk_full", 4), sig("sq_ready", 4)
        qk_split = sig("qk_split", 8)
        norm_mm, norm_full, norm_split = sig("norm_mm", 1), sig("norm_full", 1), sig("norm_split", 2)
        moved = [sig("moved0", 2 * 24 * 16), sig("moved1", 2 * 24 * 16)]
        norm_moved = sig("norm_moved", 16 * 16)
        v_ps, v_done = sig("v_ps", 2), sig("v_done", 2)
        proj_ps, exp_done = sig("proj_ps", PAIRS * TILES), sig("exp_done", PAIRS * TILES)
        a_ps, am_done = sig("a_ps", H), sig("am_done", H)
        prod_ps, d_ps = sig("prod_ps", GROUPS), sig("d_ps", GROUPS)
        copied = [sig("copied0", GROUPS), sig("copied1", GROUPS)]
        s_step, read_ps = sig("s_step", (NT + 1) * GROUPS), sig("read_ps", GROUPS)
        oT_added, o_ps, y_step = sig("oT_added", GROUPS), sig("o_ps", GROUPS), sig("y_step", 3 * GROUPS)
        mod2_set = sig("mod2_set", 1)
        yT_ps, yT_done, prj_ps = sig("yT_ps", 2), sig("yT_done", 2), sig("prj_ps", 2)
        xr_loaded, xr_biased, x2_step = sig("xr_loaded", 16), sig("xr_biased", 1), sig("x2_step", 4)
        ln2_vec, ln2_pool, h2n_ready = sig("ln2_vec", 9), sig("ln2_pool", 2), sig("h2n_ready", 4)
        h2_ps, h2_full, h2_parts = sig("h2_ps", 2), sig("h2_full", 2), sig("h2_parts", 4)
        lg_ps, lg_done, lt_ps = sig("lg_ps", 1), sig("lg_done", 1), sig("lt_ps", 1)
        low_split, low_masked = sig("low_split", 2), sig("low_masked", 2)
        rt, rt_exp, mask_ps, rho_done = sig("rt", 24), sig("rt_exp", 1), sig("mask_ps", 3), sig("rho_done", 1)
        z1_ps, r1_done, z2_ps = sig("z1_ps", FT), sig("r1_done", FT), sig("z2_ps", FT)
        g_step, wo_mm, fin = sig("g_step", 2 * FT), sig("wo_mm", FT), sig("fin", 6)
        out_done = sig("out_done", 32)

        x_rows = x.rearrange("b (n t p) c -> (b n) p t c", p=P, t=NT)
        out_rows = out.rearrange("b (n t p) c -> (b n) p t c", p=P, t=NT)

        def block_rows(rows, n):
            return rows[n] if isinstance(n, int) else rows[bass.ds(n, 1)].rearrange("o p t c -> p (o t) c")

        def over_tiles(row, k):
            return row.rearrange("p (o w) -> p o w", o=1).broadcast_to([P, k, row.shape[1]])

        def last_bc(ap, k):
            return ap.broadcast_to([ap.shape[0], ap.shape[1], k])

        block = ctx.enter_context(nc.Block())

        @block.sync
        def _(sp):
            def move(dst, src):
                return sp.dma_start(dst.bitcast(F32), src.bitcast(F32))

            first = [
                (const[:], consts), (tok[:], x_rows[0]),
                (wa_raw[0], w_attn[0:P, :]), (wa_raw[1], w_attn[P:C, :]),
                (wmod_raw[0], wmod[0:P, :]), (wmod_raw[1], wmod[P:C, :]),
                (om_f[:], omega), (nrow_f[:], norm_rows),
                (qk_bias[:], b_attn[0:2 * C].rearrange("(j p) -> p j", p=P)),
                (v_bias[:], b_attn[2 * C:3 * C].rearrange("(o c) -> o c", o=1).broadcast_to([P, C])),
                (bp_row[:], b_proj.rearrange("(o c) -> o c", o=1).broadcast_to([P, C])),
                (bg_row[:], bg.rearrange("(o c) -> o c", o=1).broadcast_to([P, E])),
            ] + [(cT[:, k, :], cond[:, k * P:(k + 1) * P].rearrange("b p -> p b")) for k in range(KT)]
            assert len(first) == FIRST_LOADS
            for dst, src in first:
                sp.dma_start(dst, src, allow_slow_non_contiguous=True).then_inc(ld_first.sem, 16)
            late = [(wi_raw[k].rearrange("p (t d) -> p t d", t=FT // 2),
                     wi.rearrange("(k t p) d -> k p t d", k=2, p=P)[k]) for k in range(2)]
            late += [(wo_raw[k], wo[k * P:(k + 1) * P, :]) for k in range(KT)]
            late += [(wp[:], w_proj.rearrange("(k p) n -> p k n", p=P))]
            late += [(lora_raw[:, :, e, :], lora_b[e].rearrange("(t p) r -> p t r", p=P)) for e in range(E)]
            assert len(late) == LATE_LOADS
            for dst, src in late:
                sp.dma_start(dst, src).then_inc(ld_late.sem, 16)
            sp.dma_start(xr[:], x_rows[0]).then_inc(xr_loaded.sem, 16)
            sp.wait_ge(set_pool.sem, 1)
            a_rows = lora_a.rearrange("e r d -> (e r) d")
            for q in range(3):
                sp.dma_start(low_raw[32 * q:32 * q + LORA, :], a_rows).then_inc(ld_low.sem, 16)
            sp.dma_start(low_raw[LOGIT_ROW:LOGIT_ROW + E, :], wg).then_inc(ld_low.sem, 16)
            sp.wait_ge(om_parts.sem, 4)
            for a in range(2):
                for k, part in enumerate((om_r, om_l, om_r)):
                    row = a * HEAD_ROWS + k * DH
                    move(omega_x[row:row + DH, a * M:(a + 1) * M], part[:]).then_inc(om_moved.sem, 16)
            move(omega_x[2 * HEAD_ROWS:XROWS, :], nrow_r[:]).then_inc(om_moved.sem, 16)
            sp.sem_inc(out_done.sem, out_done.per)

            def front_moves(n):
                for j in range(4):
                    kind, half = j // 2, j % 2
                    for part in range(2):
                        wait(sp, qk_split, n, 2 * j + part + 1)
                        src = (qk_r, qk_l)[part]
                        for h in range(PAIRS):
                            pair, a = half * 4 + h // 2, h % 2
                            for k in ((0, 1), (2,))[part]:
                                row = a * HEAD_ROWS + k * DH
                                move(xq[row:row + DH, kind, pair, :],
                                     src[h * DH:(h + 1) * DH, j % 2, :]).then_inc(moved[j % 2].sem, 16)
                wait(sp, norm_split, n, 2)
                for part, src in enumerate((norm_r, norm_l)):
                    for j in range(4):
                        kind, half = j // 2, j % 2
                        for a in range(2):
                            row = 2 * HEAD_ROWS + 2 * part + a
                            p0 = j * VA + a * GROUP
                            move(xq[row:row + 1, kind, half * GROUP:(half + 1) * GROUP, :],
                                 src[p0:p0 + GROUP, :]).then_inc(norm_moved.sem, 16)

            def ffn_stores(n):
                dst = block_rows(out_rows, n)
                for b in range(2):
                    wait(sp, fin, n, 3 * b + 3)
                    sp.dma_start(dst[:, 2 * b:2 * b + 2, :],
                                 tg[:, b, :].rearrange("p (t c) -> p t c", t=2)).then_inc(out_done.sem, 16)

            front_moves(0)
            with sp.Fori(0, NB - 1) as i:
                wait(sp, tok_free, i, 1)
                sp.dma_start(tok[:], block_rows(x_rows, i + 1)).then_inc(x_loaded.sem, 16)
                front_moves(i + 1)
                ffn_stores(i)
                sp.dma_start(xr[:], block_rows(x_rows, i + 1)).then_inc(xr_loaded.sem, 16)
            ffn_stores(NB - 1)
            wait(sp, out_done, NB, out_done.per)

        @block.tensor
        def _(pe):
            def split3(dst, w_r, w_l, v_r, v_l, first, last):
                pe.matmul(dst, w_r, v_r, start=first, stop=False)
                pe.matmul(dst, w_l, v_r, start=False, stop=False)
                return pe.matmul(dst, w_r, v_l, start=False, stop=last)

            def setup_mods():
                pe.wait_ge(ld_first.sem, 16 * FIRST_LOADS)
                pe.wait_ge(set_vec.sem, 4)
                for m, which in enumerate((1, 0, 4, 3)):
                    for half in range(KT):
                        col = (m * KT + half) * B
                        for k in range(KT):
                            pe.matmul(pa[0][:, col:col + B],
                                      wmod_raw[k][:, which * C + half * P:which * C + half * P + P],
                                      sT[:, k, :], start=k == 0, stop=k == KT - 1)
                for which, dst in ((2, pb[0]), (5, pb[1])):
                    for b in range(B):
                        for k in range(KT):
                            mm = pe.matmul(dst[:, b * C:(b + 1) * C], s_rep[:, k, b, :],
                                           wmod_raw[k][:, which * C:(which + 1) * C],
                                           start=k == 0, stop=k == KT - 1)
                mm.then_inc(set_pe.sem, 1)

            def transpose1(n):
                wait(pe, hn_ready, n, NT)
                for k in range(KT):
                    for t in range(NT):
                        mm = pe.transpose(ring[k][:, t * P:(t + 1) * P], tok[:, t, k * P:(k + 1) * P], ident)
                    mm.then_inc(hT_ps.sem, 1)

            def qk(n, j):
                if j == 0:
                    wait(pe, hT_parts, n, 4)
                for k in range(KT):
                    w = slice(j * P, (j + 1) * P)
                    mm = split3(qk_bank[j][:], wa_r[:, k, w], wa_l[:, k, w], h_r[:, k, :], h_l[:, k, :],
                                k == 0, k == KT - 1)
                mm.then_inc(qk_ps.sem, 1)

            def norms(n):
                wait(pe, sq_ready, n, 4)
                for j in range(4):
                    mm = pe.matmul(pa[0][j * VA:(j + 1) * VA, :], headsum, qk_sq[:, j, :], start=True, stop=True)
                mm.then_inc(norm_mm.sem, 1)

            def values(n):
                for t in range(NT):
                    dst = pb[t // 2][:, t % 2 * C:(t % 2 + 1) * C]
                    tt = slice(t * P, (t + 1) * P)
                    for k in range(KT):
                        mm = split3(dst, h_r[:, k, tt], h_l[:, k, tt],
                                    wa_r[:, k, 2 * C:3 * C], wa_l[:, k, 2 * C:3 * C], k == 0, k == KT - 1)
                    if t % 2:
                        mm.then_inc(v_ps.sem, 1)

            def setup_late():
                pe.wait_ge(ld_late.sem, 16 * LATE_LOADS)
                wait(pe, v_done, 0, 2)
                wait(pe, norm_full, 0, 1)
                for k in range(KT):
                    for half in range(2):
                        for t in range(4):
                            mm = pe.transpose(ring[2 * k + half][:, t * P:(t + 1) * P],
                                              wi_raw[half][:, t * C + k * P:t * C + (k + 1) * P], ident)
                        mm.then_inc(late_pe.sem, 1)
                for q in range(4):
                    for t in range(2):
                        for k in range(KT):
                            f = (2 * q + t) * P
                            mm = pe.transpose((*pa, *pb)[q][:, (t * KT + k) * P:(t * KT + k + 1) * P],
                                              wo_raw[k][:, f:f + P], ident)
                    mm.then_inc(late_pe.sem, 1)
                pe.wait_ge(ld_low.sem, 16 * 4)
                pe.wait_ge(late_vec.sem, 2)
                for k in range(KT):
                    mm = pe.transpose(ring[0][:, k * P:(k + 1) * P], low_raw[:, k * P:(k + 1) * P], ident)
                mm.then_inc(late_pe.sem, 1)
                pe.wait_ge(set_pool.sem, 9)
                pe.wait_ge(late_vec.sem, 6)
                for half, src in enumerate((mk1, mk2)):
                    for t in range(4):
                        mm = pe.transpose(ring[1 + half][0:LROWS, t * P:(t + 1) * P], src[:, t, :], ident)
                    mm.then_inc(late_pe.sem, 1)
                pe.wait_ge(late_vec.sem, 12)
                pe.wait_ge(late_act.sem, 5)

            def features(n, p):
                if p == 0:
                    wait(pe, moved[0], n, moved[0].per)
                    wait(pe, moved[1], n, moved[1].per)
                    wait(pe, norm_moved, n, norm_moved.per)
                for k in range(TILES):
                    tile = p * TILES + k
                    dst = ring[tile % 4]
                    if tile >= 4:
                        wait(pe, exp_done, n, tile - 3)
                    if k < 4:
                        mm = pe.matmul(dst[:], omega_x[:, k // 2 * M:(k // 2 + 1) * M], xq[:, k % 2, p, :],
                                       start=True, stop=True)
                    else:
                        for c in range(2):
                            t = (2 * (k - 4) + c) * P
                            mm = pe.matmul(dst[:, c * 2 * M:(c + 1) * 2 * M], xq[:, 1, p, t:t + P], omega_x[:],
                                           start=True, stop=True)
                    mm.then_inc(proj_ps.sem, 1)

            def scores(n, q, a):
                wait(pe, exp_done, n, q * TILES + 2 * a + 2)
                if q:
                    wait(pe, am_done, n, 2 * (q - 1) + a + 1)
                for c in range(NT):
                    tt = slice(c * P, (c + 1) * P)
                    mm = pe.matmul(pa[a][:, tt], phkT[:, q % 2, a, tt], phq[:, q // 2 % 2, 2 * (q % 2) + a, tt],
                                   start=True, stop=True)
                mm.then_inc(a_ps.sem, 1)

            def products(n, gr):
                if gr == 0:
                    wait(pe, v_done, n, 2)
                else:
                    wait(pe, y_step, n, 3 * gr)
                wait(pe, am_done, n, GROUP * (gr + 1))
                wait(pe, exp_done, n, 2 * TILES * (gr + 1))
                for j in range(GROUP):
                    rows = slice(j * VA, (j + 1) * VA)
                    for c in range(NT):
                        both = am_phk[:, 0:2 + gr % 2:1 + gr % 2, j, c * P:(c + 1) * P]
                        mm = pe.matmul(prod[rows, c], v_ones[:, c, GROUP * gr + j, :], both, start=True, stop=True)
                mm.then_inc(prod_ps.sem, 1)

            def state_transpose(n, gr):
                for c in range(NT):
                    if c % 2 == 0:
                        wait(pe, copied[c // 2], n, gr + 1)
                    mm = pe.transpose(prod[:, c, 1, :], prod_sb[:, c, 1, :], ident)
                mm.then_inc(d_ps.sem, 1)

            def state_reads(n, gr):
                wait(pe, s_step, n, (NT + 1) * (gr + 1))
                for j in range(GROUP):
                    rows = slice(j * VA, (j + 1) * VA)
                    for c in range(NT):
                        mm = pe.matmul(prod[rows, c, 1, :], s_sb[:, c, rows], phq[:, gr % 2, j, c * P:(c + 1) * P],
                                       start=True, stop=True)
                mm.then_inc(read_ps.sem, 1)

            def out_transpose(n, gr):
                wait(pe, oT_added, n, gr + 1)
                for c in range(NT):
                    mm = pe.transpose(prod[:, c, 0, :], oT_sb[:, c, :], ident)
                mm.then_inc(o_ps.sem, 1)

            def attend(n, front_next):
                features(n, 0)
                features(n, 1)
                wait(pe, mod2_set, n, 1)
                scores(n, 0, 0)
                scores(n, 0, 1)
                features(n, 2)
                scores(n, 1, 0)
                scores(n, 1, 1)
                features(n, 3)
                for gr in range(GROUPS):
                    more, last = gr + 1 < GROUPS, gr + 1 == GROUPS
                    q = 2 * gr + 2
                    products(n, gr)
                    if more:
                        scores(n, q, 0)
                    elif front_next:
                        transpose1(n + 1)
                    state_transpose(n, gr)
                    if more:
                        scores(n, q, 1)
                        scores(n, q + 1, 0)
                    state_reads(n, gr)
                    if gr + 2 < GROUPS:
                        features(n, q + 2)
                    if last and front_next:
                        qk(n + 1, 0)
                        qk(n + 1, 1)
                    out_transpose(n, gr)
                    if more:
                        scores(n, q + 1, 1)
                    if gr + 2 < GROUPS:
                        features(n, q + 3)

            def y_transpose(n):
                wait(pe, y_step, n, 3 * GROUPS)
                for k in range(KT):
                    for t in range(NT):
                        mm = pe.transpose(ring[k][:, t * P:(t + 1) * P], y[:, t, k * P:(k + 1) * P], ident)
                    mm.then_inc(yT_ps.sem, 1)

            def projection(n):
                wait(pe, yT_done, n, KT)
                for t in range(NT):
                    dst = (pa[1], ring[2])[t // 2][:, t % 2 * C:(t % 2 + 1) * C]
                    for k in range(KT):
                        mm = pe.matmul(dst, yT[:, k, t * P:(t + 1) * P], wp[:, k, :], start=k == 0, stop=k == KT - 1)
                    if t % 2:
                        mm.then_inc(prj_ps.sem, 1)

            def base(n, f):
                if f == 0:
                    wait(pe, h2_parts, n, 4)
                if f >= 4:
                    wait(pe, g_step, n, 2 * (f - 4) + 1)
                w = slice(f * P, (f + 1) * P)
                for k in range(KT):
                    split3(z_bank[f % 4][:], wi_r[:, k, w], wi_l[:, k, w], h_r[:, k, :], h_l[:, k, :], k == 0, False)

            def ffn_head(n, front_next):
                wait(pe, h2n_ready, n, NT)
                for k, dst in enumerate((ring[3], ring[0])):
                    for t in range(NT):
                        mm = pe.transpose(dst[:, t * P:(t + 1) * P], tok[:, t, k * P:(k + 1) * P], ident)
                    mm.then_inc(h2_ps.sem, 1)
                wait(pe, h2_full, n, KT)
                for k in range(KT):
                    mm = pe.matmul(ring[1][:], low_t[:, k, :], h_f[:, k, :], start=k == 0, stop=k == KT - 1)
                    if k == 0:
                        mm.then_inc(tok_free.sem, 1)
                mm.then_inc(lg_ps.sem, 1)
                base(n, 0)
                wait(pe, lg_done, n, 1)
                if front_next:
                    wait(pe, norm_full, n + 1, 1)
                base(n, 1)
                rows = slice(LOGIT_ROW, LOGIT_ROW + E)
                for t in range(NT):
                    mm = pe.transpose(pa[0][:, t * E:(t + 1) * E], lg[rows, t * P:(t + 1) * P], ident[rows, rows])
                mm.then_inc(lt_ps.sem, 1)
                base(n, 2)

            def masks(n):
                for q, (src, w, need, dst) in enumerate(((mk1, LROWS, 18, pa[1]), (mk2, LROWS, 21, pb[0]),
                                                         (None, P, 22, pb[1]))):
                    wait(pe, rt, n, need)
                    for t in range(NT):
                        tile = src[:, t, :] if src is not None else r2[:, 0, t * P:(t + 1) * P]
                        mm = pe.transpose(dst[0:w, t * P:(t + 1) * P], tile, ident)
                    mm.then_inc(mask_ps.sem, 1)

            def experts(n):
                for f in range(FT + 3):
                    if f < FT:
                        if f == 0:
                            wait(pe, low_masked, n, 2)
                        w = slice(f * P, (f + 1) * P)
                        pe.matmul(z_bank[f % 4][:], lora_w[:, w], low1[:], start=False,
                                  stop=True).then_inc(z1_ps.sem, 1)
                    if 3 <= f + 2 < FT:
                        base(n, f + 2)
                    if 1 <= f <= FT:
                        wait(pe, r1_done, n, f)
                        w = slice((f - 1) * P, f * P)
                        pe.matmul(z_bank[(f - 1) % 4][:], lora_w[:, w], low2[:], start=False, stop=True,
                                  skip_group_check=True).then_inc(z2_ps.sem, 1)
                    if f >= 3:
                        k = f - 3
                        wait(pe, g_step, n, 2 * k + 2)
                        for t in range(NT):
                            mm = pe.matmul(pa[t // 2][:, t % 2 * C:(t % 2 + 1) * C], g[:, k % 3, t * P:(t + 1) * P],
                                           wo_t[:, k, :], start=k == 0 and t % 2 == 0, stop=k == FT - 1,
                                           skip_group_check=True)
                        mm.then_inc(wo_mm.sem, 1)

            setup_mods()
            transpose1(0)
            pe.wait_ge(set_vec.sem, SETUP_VEC)
            for j in range(4):
                qk(0, j)
            norms(0)
            values(0)
            setup_late()
            pe.wait_ge(om_moved.sem, 16 * 7)
            pe.nop().then_inc(tok_free.sem, 1)

            def after_attend(n, front_next):
                if front_next:
                    qk(n + 1, 2)
                    qk(n + 1, 3)
                y_transpose(n)
                if front_next:
                    norms(n + 1)
                projection(n)
                if front_next:
                    values(n + 1)
                ffn_head(n, front_next)
                masks(n)
                experts(n)

            with pe.Fori(0, NB - 1) as i:
                attend(i, True)
                after_attend(i, True)
            attend(NB - 1, False)
            after_attend(NB - 1, False)

        @block.scalar
        def _(act):
            def setup():
                act.wait_ge(ld_first.sem, 16 * FIRST_LOADS)
                act.activation(sT[:], cT[:], ACT.Exp, scale=-1.0).then_inc(set_act.sem, 1)
                act.activation(qk_bias[:], qk_bias[:], ACT.Copy, scale=Q_SCALE).then_inc(set_act.sem, 1)

            def front_hT(n):
                wait(act, ln1_vec, n, 9)
                for k in range(KT):
                    wait(act, hT_ps, n, k + 1)
                    act.activation(h_f[:, k, :], ring[k][:], ACT.Identity, bias=mod1_now[:, KT + k:KT + k + 1],
                                   scale=mod1_now[:, k:k + 1]).then_inc(hT_full.sem, 1)

            def front_qk(n, j):
                wait(act, qk_ps, n, j + 1)
                if j >= 2:
                    wait(act, qk_split, n, 2 * (j - 2) + 2)
                act.activation(qk_f[:, j % 2, :], qk_bank[j][:], ACT.Identity, bias=qk_bias[:, j:j + 1],
                               scale=Q_SCALE).then_inc(qk_full.sem, 1)
                act.activation(qk_sq[:, j, :], qk_bank[j][:], ACT.Square, bias=qk_bias[:, j:j + 1],
                               scale=Q_SCALE).then_inc(sq_ready.sem, 1)

            def front_norm(n):
                wait(act, norm_mm, n, 1)
                wait(act, qk_split, n, 6)
                act.activation(qk_f[:, 0, :], pa[0][:], ACT.Copy).then_inc(norm_full.sem, 1)

            def setup_late():
                for q in range(4):
                    act.wait_ge(late_pe.sem, 5 + q)
                    act.activation(wo_t[:, 2 * q:2 * q + 2, :].rearrange("p t c -> p (t c)"), (*pa, *pb)[q][:],
                                   ACT.Copy).then_inc(late_act.sem, 1)
                act.wait_ge(late_pe.sem, 9)
                act.activation(low_t[:].rearrange("p k m -> p (k m)"), ring[0][:, 0:KT * P],
                               ACT.Copy).then_inc(late_act.sem, 1)

            def features(n, q, tiles):
                for k in tiles:
                    tile = q * TILES + k
                    wait(act, proj_ps, n, tile + 1)
                    slot = q // 2 % 2
                    if k >= 4:
                        c = 2 * (k - 4) * P
                        dst = am_phk[:, 1 + slot, 2 * (q % 2):2 * (q % 2) + 2, c:c + 2 * P]\
                            .rearrange("p a (c m) -> p c a m", c=2)
                        src = ring[tile % 4][:].rearrange("p (c a m) -> p c a m", c=2, a=2)
                    else:
                        dst = (phq[:, slot, 2 * (q % 2) + k // 2, :], phkT[:, q % 2, k // 2, :])[k % 2]
                        src = ring[tile % 4][:]
                    act.activation(dst, src, ACT.Exp).then_inc(exp_done.sem, 1)

            def attend(n, front_next):
                for q in range(3):
                    features(n, q, range(TILES))
                for gr in range(GROUPS):
                    ahead = 2 * gr + 3
                    if ahead < PAIRS:
                        features(n, ahead, range(4))
                    wait(act, prod_ps, n, gr + 1)
                    act.activation(prod_sb[:, 0:2].rearrange("p c k m -> p (c k m)"), pb[0],
                                   ACT.Copy).then_inc(copied[0].sem, 1)
                    if ahead < PAIRS:
                        features(n, ahead, range(4, TILES))
                    if ahead + 1 < PAIRS:
                        features(n, ahead + 1, range(TILES))
                if front_next:
                    front_hT(n + 1)

            def y_copy(n):
                for k in range(KT):
                    wait(act, yT_ps, n, k + 1)
                    act.activation(yT[:, k, :], ring[k][:], ACT.Copy).then_inc(yT_done.sem, 1)

            def ffn(n):
                for k, src in enumerate((ring[3], ring[0])):
                    wait(act, h2_ps, n, k + 1)
                    act.activation(h_f[:, k, :], src[:], ACT.Identity,
                                   bias=mod2_cols[:, KT + k:KT + k + 1],
                                   scale=mod2_cols[:, k:k + 1]).then_inc(h2_full.sem, 1)
                wait(act, lg_ps, n, 1)
                act.activation(lg, ring[1][:], ACT.Copy).then_inc(lg_done.sem, 1)
                wait(act, rt, n, 10)
                act.activation(exo[:], ex[:], ACT.Exp).then_inc(rt_exp.sem, 1)
                wait(act, mask_ps, n, 3)
                act.activation(rho, pb[1], ACT.Copy).then_inc(rho_done.sem, 1)
                for f in range(FT):
                    wait(act, z1_ps, n, f + 1)
                    if f >= 3:
                        wait(act, wo_mm, n, f - 2)
                    act.activation(g[:, f % 3, :], z_bank[f % 4][:], ACT.Relu).then_inc(r1_done.sem, 1)

            setup()
            act.wait_ge(set_act.sem, 2)
            front_hT(0)
            for j in range(4):
                front_qk(0, j)
            front_norm(0)
            setup_late()

            def after_attend(n, front_next):
                if front_next:
                    for j in range(4):
                        front_qk(n + 1, j)
                y_copy(n)
                if front_next:
                    front_norm(n + 1)
                ffn(n)

            with act.Fori(0, NB - 1) as i:
                attend(i, True)
                after_attend(i, True)
            attend(NB - 1, False)
            after_attend(NB - 1, False)

        @block.vector
        def _(dve):
            setup_count = [0]

            def step(ins):
                setup_count[0] += 1
                ins.then_inc(set_vec.sem, 1)
                dve.wait_ge(set_vec.sem, setup_count[0])

            def setup():
                dve.wait_ge(set_act.sem, 1)
                step(dve.tensor_scalar(ex[:, 0, 0:KT * B], sT[:].rearrange("p k b -> p (k b)"), 1.0, None, ALU.add))
                step(dve.reciprocal(exo[:, 0, 0:KT * B], ex[:, 0, 0:KT * B]))
                step(dve.tensor_tensor(sT[:].rearrange("p k b -> p (k b)"), cT[:].rearrange("p k b -> p (k b)"),
                                       exo[:, 0, 0:KT * B], ALU.mult))
                step(dve.tensor_copy(s_rep.rearrange("p k b m -> p (k b) m"),
                                     last_bc(sT[:].rearrange("p k (b o) -> p (k b) o", o=1), P)))
                dve.tensor_copy(om_r[:], om_f[:]).then_inc(om_parts.sem, 1)
                dve.tensor_copy(nrow_r[:], nrow_f[:]).then_inc(om_parts.sem, 1)
                dve.memset(omega_x[:].bitcast(F32), 0.0).then_inc(om_parts.sem, 1)
                dve.wait_ge(om_parts.sem, 1)
                dve.tensor_tensor(om_l[:], om_f[:], om_r[:].bitcast(F32), ALU.subtract).then_inc(om_parts.sem, 1)
                for k in range(KT):
                    step(dve.tensor_copy(wa_r[:, k, :], wa_raw[k]))
                    step(dve.tensor_tensor(wa_l[:, k, :], wa_raw[k], wa_r[:, k, :].bitcast(F32), ALU.subtract))
                dve.wait_ge(set_pe.sem, 1)
                cols_ps = pa[0][:, 0:8 * B].rearrange("p (m b) -> p b m", b=B)
                step(dve.tensor_scalar(mod1[:, :, 0:KT], cols_ps[:, :, 0:2], 1.0, None, ALU.add))
                step(dve.tensor_copy(mod1[:, :, KT:2 * KT], cols_ps[:, :, 2:4]))
                step(dve.tensor_scalar(mod2[:, :, 3 * C:3 * C + KT], cols_ps[:, :, 4:6], 1.0, None, ALU.add))
                step(dve.tensor_copy(mod2[:, :, 3 * C + KT:3 * C + 2 * KT], cols_ps[:, :, 6:8]))
                for q, src in enumerate(pb):
                    rows = src.rearrange("p (b c) -> p b c", b=B)
                    gate = mod2[:, :, q * C:(q + 1) * C]
                    tmp = y[:, 0:2, :]
                    step(dve.tensor_copy(tmp, rows))
                    step(dve.scalar_tensor_tensor(gate, tmp, -1.0, tmp, ALU.mult, ALU.max))
                    step(dve.tensor_scalar(gate, gate, 0.25, None, ALU.max))
                    step(dve.tensor_scalar(tmp, tmp, 0.0, 2.0, ALU.is_ge, ALU.mult))
                    step(dve.scalar_tensor_tensor(gate, tmp, -1.0, gate, ALU.add, ALU.mult))
                step(dve.tensor_tensor(mod2[:, :, 2 * C:3 * C], mod2[:, :, 0:C], over_tiles(bp_row[:], B), ALU.mult))
                step(dve.memset(neg_half[:], -0.5))
                step(dve.memset(eps[:], EPS_LN))
                step(dve.memset(state[:], 0.0))
                step(dve.memset(v_ones[:, :, :, DH:VA], 1.0))
                assert setup_count[0] == SETUP_VEC

            def statistics(n, src, vec):
                for t in range(NT):
                    dve.bn_stats(stats[:, t, :], src[:, t, :]).then_inc(vec.sem, 1)
                wait(dve, vec, n, NT)
                row = n // BLOCKS_PER_ROW
                row_mod1 = mod1[:, row, :] if isinstance(n, int) else \
                    mod1[:, bass.ds(row, 1), :].rearrange("p o c -> p (o c)")
                row_mod2 = mod2[:, row, 3 * C:] if isinstance(n, int) else \
                    mod2[:, bass.ds(row, 1), 3 * C:].rearrange("p o c -> p (o c)")
                dve.tensor_copy(*((mod1_now[:], row_mod1) if vec is ln1_vec else (mod2_cols[:], row_mod2)))\
                    .then_inc(vec.sem, 1)
                for t in range(NT):
                    dve.bn_aggr(mv[:, t, :], stats[:, t, :]).then_inc(vec.sem, 1)

            def normalize_apply(n, src, pool, ready):
                wait(dve, pool, n, 2)
                for t in range(NT):
                    dve.tensor_scalar(tok[:, t, :], src[:, t, :], mv[:, t, 0:1], rstd[:, t:t + 1],
                                      ALU.subtract, ALU.mult).then_inc(ready.sem, 1)

            def ln1_stats(n, first):
                if first:
                    dve.wait_ge(ld_first.sem, 16 * FIRST_LOADS)
                else:
                    wait(dve, x_loaded, n - 1, 16)
                statistics(n, tok, ln1_vec)

            def split_h(n, full, parts):
                for k in range(KT):
                    wait(dve, full, n, k + 1)
                    dve.tensor_copy(h_r[:, k, :], h_f[:, k, :]).then_inc(parts.sem, 1)
                    wait(dve, parts, n, 2 * k + 1)
                    dve.tensor_tensor(h_l[:, k, :], h_f[:, k, :], h_r[:, k, :].bitcast(F32),
                                      ALU.subtract).then_inc(parts.sem, 1)

            def split_qk(n, j):
                wait(dve, qk_full, n, j + 1)
                if j >= 2:
                    wait(dve, moved[j % 2], n, 24 * 16)
                dve.tensor_copy(qk_r[:, j % 2, :], qk_f[:, j % 2, :]).then_inc(qk_split.sem, 1)
                wait(dve, qk_split, n, 2 * j + 1)
                dve.tensor_tensor(qk_l[:, j % 2, :], qk_f[:, j % 2, :], qk_r[:, j % 2, :].bitcast(F32),
                                  ALU.subtract).then_inc(qk_split.sem, 1)

            def split_norm(n):
                wait(dve, norm_full, n, 1)
                dve.tensor_copy(norm_r[:], qk_f[:, 0, :]).then_inc(norm_split.sem, 1)
                wait(dve, norm_split, n, 1)
                dve.tensor_tensor(norm_l[:], qk_f[:, 0, :], norm_r[:].bitcast(F32),
                                  ALU.subtract).then_inc(norm_split.sem, 1)

            def values(n):
                for b in range(2):
                    wait(dve, v_ps, n, b + 1)
                    dve.tensor_tensor(v_ones[:, 2 * b:2 * b + 2, :, 0:DH],
                                      pb[b].rearrange("p (t h d) -> p t h d", t=2, d=DH),
                                      over_tiles(v_bias[:], 2).rearrange("p t (h d) -> p t h d", d=DH),
                                      ALU.add).then_inc(v_done.sem, 1)

            def setup_late():
                for k in range(KT):
                    for half in range(2):
                        q = 2 * k + half
                        dve.wait_ge(late_pe.sem, q + 1)
                        w = slice(half * T, (half + 1) * T)
                        dve.tensor_copy(wi_r[:, k, w], ring[q][:]).then_inc(late_vec.sem, 1)
                        dve.wait_ge(late_vec.sem, 2 * q + 1)
                        dve.tensor_tensor(wi_l[:, k, w], ring[q][:], wi_r[:, k, w].bitcast(F32),
                                          ALU.subtract).then_inc(late_vec.sem, 1)
                for half in range(2):
                    dve.wait_ge(late_pe.sem, 10 + half)
                    w = slice(half * T, (half + 1) * T)
                    dve.tensor_copy(lora_w[:, w], ring[1 + half][0:LROWS, :]).then_inc(late_vec.sem, 1)
                    dve.wait_ge(late_vec.sem, 9 + 2 * half)
                    dve.tensor_tensor(lora_w[32:64, w], ring[1 + half][32:64, :], lora_w[32:64, w].bitcast(F32),
                                      ALU.subtract).then_inc(late_vec.sem, 1)

            def causal_scores(n, q, a):
                wait(dve, a_ps, n, 2 * q + a + 1)
                dve.tensor_tensor(am[:, 2 * (q % 2) + a, :].rearrange("p (c t) -> p c t", c=NT),
                                  pa[a][:].rearrange("p (c t) -> p c t", c=NT),
                                  over_tiles(causal, NT), ALU.min).then_inc(am_done.sem, 1)

            def advance_state(n, gr):
                fresh = (n % BLOCKS_PER_ROW + BLOCKS_PER_ROW - 1) // BLOCKS_PER_ROW
                start = state[:, fresh, gr, :] if isinstance(n, int) else \
                    state[:, bass.ds(fresh, 1), gr, :].rearrange("p o m -> p (o m)")
                c0 = (NT + 1) * gr
                wait(dve, d_ps, n, gr + 1)
                dve.tensor_copy(s_sb[:, 0, :], start).then_inc(s_step.sem, 1)
                for c in range(NT):
                    wait(dve, s_step, n, c0 + c + 1)
                    after = s_sb[:, c + 1, :] if c + 1 < NT else state[:, 1, gr, :]
                    dve.tensor_tensor(after, s_sb[:, c, :], prod[:, c, 1, :], ALU.add).then_inc(s_step.sem, 1)

            def add_reads(n, gr):
                wait(dve, read_ps, n, gr + 1)
                dve.tensor_tensor(oT_sb[:], prod_sb[:, :, 0, :], prod[:, :, 1, :], ALU.add).then_inc(oT_added.sem, 1)

            def divide(n, gr):
                wait(dve, o_ps, n, gr + 1)
                o = prod[:, :, 0, :].rearrange("p c (j d) -> p c j d", j=GROUP)
                dve.tensor_scalar(den[:], o[:, :, :, DH], EPS_DEN, None, ALU.add).then_inc(y_step.sem, 1)
                wait(dve, y_step, n, 3 * gr + 1)
                dve.reciprocal(rden[:], den[:]).then_inc(y_step.sem, 1)
                wait(dve, y_step, n, 3 * gr + 2)
                dve.tensor_tensor(y[:, :, gr * GROUP * DH:(gr + 1) * GROUP * DH]
                                  .rearrange("p c (j d) -> p c j d", j=GROUP), o[:, :, :, 0:DH],
                                  rden[:].rearrange("p c (j o) -> p c j o", o=1).broadcast_to([P, NT, GROUP, DH]),
                                  ALU.mult).then_inc(y_step.sem, 1)

            def attend(n, front_next):
                for q in range(2):
                    for a in range(2):
                        causal_scores(n, q, a)
                for gr in range(GROUPS):
                    more = gr + 1 < GROUPS
                    q = 2 * gr + 2
                    wait(dve, prod_ps, n, gr + 1)
                    dve.tensor_copy(prod_sb[:, 2:4].rearrange("p c k m -> p (c k m)"), pb[1])\
                        .then_inc(copied[1].sem, 1)
                    if more:
                        causal_scores(n, q, 0)
                    advance_state(n, gr)
                    if more:
                        causal_scores(n, q, 1)
                        causal_scores(n, q + 1, 0)
                    elif front_next:
                        split_h(n + 1, hT_full, hT_parts)
                    add_reads(n, gr)
                    divide(n, gr)
                    if more:
                        causal_scores(n, q + 1, 1)
                    if front_next and gr == 0:
                        ln1_stats(n + 1, False)
                    if front_next and gr == 1:
                        normalize_apply(n + 1, tok, ln1_pool, hn_ready)

            def residual(n):
                wait(dve, out_done, n, out_done.per)
                wait(dve, mod2_set, n, 1)
                for b, src in enumerate((pa[1], ring[2])):
                    wait(dve, prj_ps, n, b + 1)
                    dve.tensor_tensor(tg[:, b, :].rearrange("p (t c) -> p t c", t=2),
                                      src[:].rearrange("p (t c) -> p t c", t=2),
                                      over_tiles(ga_now, 2), ALU.mult).then_inc(x2_step.sem, 1)
                wait(dve, xr_biased, n, 1)
                for b in range(2):
                    wait(dve, x2_step, n, b + 1)
                    two = xr[:, 2 * b:2 * b + 2, :].rearrange("p t c -> p (t c)")
                    dve.tensor_tensor(two, tg[:, b, :], two, ALU.add).then_inc(x2_step.sem, 1)
                wait(dve, x2_step, n, 4)

            def router(n):
                count = [0]

                def link(ins):
                    count[0] += 1
                    ins.then_inc(rt.sem, 1)

                def after(c=None):
                    wait(dve, rt, n, c or count[0])

                wait(dve, lg_done, n, 1)
                dve.tensor_copy(low[:], lg[0:LROWS]).then_inc(low_split.sem, 1)
                wait(dve, low_split, n, 1)
                dve.tensor_tensor(low[64:96, :], lg[64:96], low[64:96, :].bitcast(F32),
                                  ALU.subtract).then_inc(low_split.sem, 1)
                wait(dve, lt_ps, n, 1)
                logit, eq, pr, one1, rest, one2, diff = (route[:, k] for k in range(7))
                m1, m2, pm = rmax[:, 0], rmax[:, 1], rmax[:, 2]
                col = lambda ap: last_bc(ap.rearrange("p (t o) -> p t o", o=1), E)
                link(dve.tensor_tensor(logit, pa[0][:, 0:NT * E].rearrange("p (t e) -> p t e", e=E),
                                       over_tiles(bg_row[:], NT), ALU.add))
                after()

                def first_of_largest(values, largest, one):
                    link(dve.tensor_tensor(eq, values, col(largest), ALU.is_equal))
                    after()
                    link(dve.tensor_tensor(pr, eq, over_tiles(prio, NT), ALU.mult))
                    after()
                    link(dve.tensor_reduce(pm, pr, AX.X, ALU.max))
                    after()
                    link(dve.tensor_tensor(one, pr, col(pm), ALU.is_equal))
                    after()

                link(dve.tensor_reduce(m1, logit, AX.X, ALU.max))
                after()
                first_of_largest(logit, m1, one1)
                link(dve.scalar_tensor_tensor(rest, one1, PAD, logit, ALU.mult, ALU.add))
                after()
                link(dve.tensor_reduce(m2, rest, AX.X, ALU.max))
                after()
                link(dve.tensor_tensor(ex[:, :, 0:E], logit, col(m1), ALU.subtract))
                link(dve.tensor_tensor(ex[:, :, E], m2, m1, ALU.subtract))
                assert count[0] == 10
                first_of_largest(rest, m2, one2)
                link(dve.tensor_tensor(diff, one2, one1, ALU.subtract))
                after()
                for mk, one in ((mk1, one1), (mk2, diff)):
                    for q in range(3):
                        link(dve.tensor_copy(mk[:, :, 32 * q:32 * q + LORA].rearrange("p t (e r) -> p t e r", r=R),
                                             one.rearrange("p t (e o) -> p t e o", o=1)
                                             .broadcast_to([P, NT, E, R])))
                wait(dve, rt_exp, n, 1)
                dve.tensor_copy(r2[:, 0, :].rearrange("p (t m) -> p t m", t=NT), last_bc(exo[:, :, E:E + 1], P))\
                   .then_inc(rt.sem, 1)
                dve.tensor_reduce(wsum[:], exo[:, :, 0:E], AX.X, ALU.add).then_inc(rt.sem, 1)
                return count

            def mask_low(n):
                for q, (dst, src) in enumerate(((low1, pa[1]), (low2, pb[0]))):
                    wait(dve, mask_ps, n, q + 1)
                    dve.tensor_tensor(dst[:], low[:].bitcast(F32), src[0:LROWS, :],
                                      ALU.mult).then_inc(low_masked.sem, 1)

            def experts(n):
                wait(dve, rho_done, n, 1)
                for f in range(FT):
                    wait(dve, z2_ps, n, f + 1)
                    dve.scalar_tensor_tensor(r2[:, f % 2, :], z_bank[f % 4][:], 0.0, rho, ALU.max,
                                             ALU.mult).then_inc(g_step.sem, 1)
                    wait(dve, g_step, n, 2 * f + 1)
                    dve.tensor_tensor(g[:, f % 3, :], g[:, f % 3, :], r2[:, f % 2, :], ALU.add).then_inc(g_step.sem, 1)

            def finish(n):
                wait(dve, wo_mm, n, FT)
                for b in range(2):
                    for t in range(2):
                        dve.scalar_tensor_tensor(tg[:, b, t * C:(t + 1) * C], pa[b][:, t * C:(t + 1) * C],
                                                 w1[:, 2 * b + t:2 * b + t + 1], gb_now, ALU.mult,
                                                 ALU.mult).then_inc(fin.sem, 1)
                    wait(dve, fin, n, 3 * b + 2)
                    dve.tensor_tensor(tg[:, b, :], tg[:, b, :],
                                      xr[:, 2 * b:2 * b + 2, :].rearrange("p t c -> p (t c)"),
                                      ALU.add).then_inc(fin.sem, 1)

            def ffn(n):
                statistics(n, xr, ln2_vec)
                normalize_apply(n, xr, ln2_pool, h2n_ready)

            def ffn_rest(n):
                split_h(n, h2_full, h2_parts)
                router(n)
                wait(dve, rt, n, 23)
                dve.reciprocal(w1[:], wsum[:]).then_inc(rt.sem, 1)
                mask_low(n)
                experts(n)
                finish(n)

            ln1_first = lambda: (ln1_stats(0, True), normalize_apply(0, tok, ln1_pool, hn_ready))
            setup()
            ln1_first()
            split_h(0, hT_full, hT_parts)
            for j in range(4):
                split_qk(0, j)
            split_norm(0)
            values(0)
            setup_late()

            def after_attend(n, front_next):
                if front_next:
                    for j in range(4):
                        split_qk(n + 1, j)
                    split_norm(n + 1)
                residual(n)
                ffn(n)
                if front_next:
                    values(n + 1)
                ffn_rest(n)

            with dve.Fori(0, NB - 1) as i:
                attend(i, True)
                after_attend(i, True)
            attend(NB - 1, False)
            after_attend(NB - 1, False)

        @block.gpsimd
        def _(pool):
            def setup():
                pool.memset(low_raw, 0.0).then_inc(set_pool.sem, 1)
                pool.memset(mk1[:], 0.0).then_inc(set_pool.sem, 1)
                pool.memset(mk2[:], 0.0).then_inc(set_pool.sem, 1)
                pool.wait_ge(ld_late.sem, 16 * LATE_LOADS)
                pool.wait_ge(set_pool.sem, 3)
                for half, mk in enumerate((mk1, mk2)):
                    for q in range(3):
                        pool.tensor_copy(mk[:, :, 32 * q:32 * q + LORA],
                                         lora_raw[:, 4 * half:4 * half + 4].rearrange("p t e r -> p t (e r)"))\
                            .then_inc(set_pool.sem, 1)

            def rstd_of(n, vec, sem):
                wait(pool, vec, n, 2 * NT + 1)
                pool.tensor_tensor(var_eps[:], mv[:, :, 1], eps[:], ALU.add).then_inc(sem.sem, 1)
                wait(pool, sem, n, 1)
                pool.tensor_tensor(rstd[:], var_eps[:], neg_half[:], ALU.pow).then_inc(sem.sem, 1)

            def attend(n, front_next):
                row = n // BLOCKS_PER_ROW
                src = mod2[:, row, 0:3 * C] if isinstance(n, int) else \
                    mod2[:, bass.ds(row, 1), 0:3 * C].rearrange("p o c -> p (o c)")
                pool.tensor_copy(mod2_now[:], src).then_inc(mod2_set.sem, 1)
                if front_next:
                    rstd_of(n + 1, ln1_vec, ln1_pool)

            def residual(n):
                wait(pool, xr_loaded, n, 16)
                wait(pool, mod2_set, n, 1)
                two = xr[:]
                pool.tensor_tensor(two, two, over_tiles(bpg_now, NT), ALU.add).then_inc(xr_biased.sem, 1)

            setup()
            pool.wait_ge(set_vec.sem, SETUP_VEC)
            rstd_of(0, ln1_vec, ln1_pool)
            with pool.Fori(0, NB - 1) as i:
                attend(i, True)
                residual(i)
                rstd_of(i, ln2_vec, ln2_pool)
                wait(pool, fin, i, 6)
            attend(NB - 1, False)
            residual(NB - 1)
            rstd_of(NB - 1, ln2_vec, ln2_pool)


FIRST_LOADS = 12 + KT
LATE_LOADS = 5 + E
SETUP_VEC = 4 + 2 * KT + 4 + 10 + 1 + 4


def constants():
    import numpy as np
    r = np.arange(P)
    ident = np.eye(P, dtype=np.float32)
    causal = np.where(r[:, None] <= r[None, :], np.finfo(np.float32).max, 0).astype(np.float32)
    headsum = np.zeros((P, VA), np.float32)
    for p in range(P):
        h = p // DH
        headsum[p, h % 2 * GROUP + h // 2] = 1
    prio = np.broadcast_to(np.arange(E, 0, -1, dtype=np.float32), (P, E))
    consts = np.concatenate([ident, causal, headsum, prio], 1)
    rows = np.zeros((4, 2 * M), np.float32)
    for part in range(2):
        for a in range(2):
            rows[2 * part + a, a * M:(a + 1) * M] = -0.5
    return {"consts": np.ascontiguousarray(consts), "norm_rows": rows}


_INS = ['L0_attn_x', 'L0_attn_W_attn', 'L0_attn_b_attn', 'L0_attn_W_proj', 'L0_attn_b_proj', 'L0_attn_omega',
        'L0_ffn_Wg', 'L0_ffn_bg', 'L0_ffn_Wi', 'L0_ffn_Wo', 'L0_ffn_A', 'L0_ffn_B', 'L0_c', 'L0_wmod',
        'consts', 'norm_rows']


def kernel(**inputs):
    import numpy as np
    import concourse.bacc as bacc
    from concourse.bass_utils import run_bass_kernel_spmd

    nc = bacc.Bacc("TRN2", target_bir_lowering=False, num_devices=1)
    inputs = {**inputs, **constants()}
    arrays, args = {}, []
    for name in _INS:
        a = np.ascontiguousarray(inputs[name])
        arrays[f"in_{name}"] = a
        args.append(nc.dram_tensor(f"in_{name}", a.shape, mybir.dt.from_np(a.dtype), kind="ExternalInput").ap())
    out = nc.dram_tensor("out_x", (B, SEQ, C), F32, kind="ExternalOutput").ap()
    build(nc, *args, out)
    r = run_bass_kernel_spmd(nc, [arrays], core_ids=[0])
    return r.results[0]["out_x"]
```

```python
from contextlib import ExitStack

import concourse.bass as bass
from concourse import mybir

P = 128
B, SEQ, C = 2, 2048, 256
H, DH, M = 16, 16, 128
F, E, R = 1024, 4, 4
T = 512
NT = T // P
KT = C // P
FT = F // P
NB = B * SEQ // T
BLOCKS_PER_ROW = SEQ // T
PAIRS = H // 2
GROUP = 4
GROUPS = H // GROUP
VA = P // GROUP
PAIR_ROWS = 2 * DH
XROWS = 3 * PAIR_ROWS + 4
LORA = E * R
LROWS = 96
LOGIT_ROW = 96
EPS_LN = 1e-5
EPS_DEN = 1e-6 * M
Q_SCALE = DH ** -0.5
TILES = 6
PAD = -3.0e38

ALU = mybir.AluOpType
ACT = mybir.ActivationFunctionType
AX = mybir.AxisListType
F32 = mybir.dt.float32
F32R = mybir.dt.float32r
BF16 = mybir.dt.bfloat16

CONSTS = {"ident": P, "causal": P, "headsum": VA, "prio": E}


class Signal:

    def __init__(self, sem, per):
        self.sem, self.per = sem, per

    def at(self, n, c):
        return n * self.per + c


def wait(eng, signal, n, c):
    eng.wait_ge(signal.sem, signal.at(n, c))


def build(nc, x, w_attn, b_attn, w_proj, b_proj, omega, wg, bg, wi, wo, lora_a, lora_b, cond, wmod,
          consts, norm_rows, out, parts_out, norms_out):
    ctx = ExitStack()
    with ctx:
        def sb(name, shape, dt=F32):
            return ctx.enter_context(nc.sbuf_tensor(name, shape, dt))

        def sig(name, per=0):
            return Signal(ctx.enter_context(nc.semaphore(name)), per)

        const = sb("const", [P, sum(CONSTS.values())])
        at, cols = 0, {}
        for name, width in CONSTS.items():
            cols[name] = const[:, at:at + width]
            at += width
        ident, causal, headsum, prio = (cols[name] for name in CONSTS)
        wa_r, wa_l = sb("wa_r", [P, KT, 3 * C], F32R), sb("wa_l", [P, KT, 3 * C], F32R)
        wi_r, wi_l = sb("wi_r", [P, KT, F], F32R), sb("wi_l", [P, KT, F], F32R)
        wo_t = sb("wo_t", [P, FT, C])
        wp_ga = sb("wp_ga", [P, B, KT, C])
        low_t = sb("low_t", [P, KT, P])
        lora_w = sb("lora_w", [LROWS, F], F32R)
        omega_x = sb("omega_x", [XROWS, 2 * M], F32R)
        om_r, om_l = sb("om_r", [DH, M], F32R), sb("om_l", [DH, M], F32R)
        nrow_r = sb("nrow_r", [4, 2 * M], F32R)
        qk_bias = sb("qk_bias", [P, 4])
        v_bias = sb("v_bias", [P, C])
        bg_row = sb("bg_row", [P, E])
        neg_half, neg_one, eps = (sb(name, [P, NT]) for name in ("neg_half", "neg_one", "eps"))
        mod1 = sb("mod1", [P, B, 2 * KT])
        mod2 = sb("mod2", [P, B, 2 * C + 2 * KT])
        mod1_now = sb("mod1_now", [P, 2 * KT])
        mod2_now = sb("mod2_now", [P, 2 * C])
        mod2_cols = sb("mod2_cols", [P, 2 * KT])
        gb_now, bpg_now = (mod2_now[:, k * C:(k + 1) * C] for k in range(2))
        cT, sT = sb("cT", [P, KT, B]), sb("sT", [P, KT, B])

        tok = sb("tok", [P, NT, C])
        xr = sb("xr", [P, NT, C])
        stats, mv = sb("stats", [P, NT, 6]), sb("mv", [P, NT, 2])
        var_eps, rstd = sb("var_eps", [P, NT]), sb("rstd", [P, NT])
        neg_mean, shift = sb("neg_mean", [P, NT]), sb("shift", [P, NT])
        h_r, h_l = sb("h_r", [P, KT, T], F32R), sb("h_l", [P, KT, T], F32R)
        qk_r, qk_l = sb("qk_r", [P, 4, T], F32R), sb("qk_l", [P, 4, T], F32R)
        norm_r, norm_l = sb("norm_r", [P, T], F32R), sb("norm_l", [P, T], F32R)
        xq = sb("xq", [XROWS, 2, PAIRS, T], F32R)
        v_ones = sb("v_ones", [P, NT, H, VA])

        phq = sb("phq", [P, 2, GROUP, T])
        phkT = sb("phkT", [P, 2, 2, T])
        am_phk = sb("am_phk", [P, 3, GROUP, T])
        am = am_phk[:, 0]
        prod_sb, oT_sb = sb("prod_sb", [P, NT, 2, P]), sb("oT_sb", [P, NT, P])
        s_sb = sb("s_sb", [P, NT, P])
        state = sb("state", [P, 2, GROUPS, P])
        den, rden = sb("den", [P, NT, GROUP]), sb("rden", [P, NT, GROUP])
        y = sb("y", [P, NT, C])

        tg = sb("tg", [P, 2, 2 * C])
        low = sb("low", [LROWS, T], F32R)
        low1, low2 = norm_r[0:LROWS], norm_l[0:LROWS]
        mk1, mk2 = sb("mk1", [P, NT, LROWS]), sb("mk2", [P, NT, LROWS])
        route = sb("route", [P, 8, NT, E])
        rmax = sb("rmax", [P, 4, NT])
        ex, exo = sb("ex", [P, NT, E + 1]), sb("exo", [P, NT, E + 1])
        wsum, w1 = sb("wsum", [P, NT]), sb("w1", [P, NT])

        qk_sq = phq[:, 0]
        g, rho = phq[:, 1], am[:, 3]
        yT = phkT[:, 0]
        r2, lg = am[:, 0:2], am[:, 2]
        h_f = am_phk[:, 1, 0:2]

        flat = lambda ap: ap.rearrange("p a t -> p (a t)")
        wmod_raw = [flat(phq[:, k])[:, 0:6 * C] for k in range(KT)]
        wa_raw = [flat(phkT[:, k])[:, 0:3 * C] for k in range(KT)]
        wi_raw = [flat(am_phk[:, 2, 2 * k:2 * k + 2]) for k in range(2)]
        wo_raw = [flat(am[:, 2 * k:2 * k + 2]) for k in range(KT)]
        low_raw = tg[:, 1, 0:C]
        om_f, nrow_f, bp_row = y[0:DH, 2, 0:M], y[0:4, 3, 0:2 * M], flat(oT_sb[:])[:, 0:C]
        wp = flat(s_sb[:]).rearrange("p (k c) -> p k c", k=KT)
        ga_rows = prod_sb[:, 1:3].rearrange("p b k m -> p b (k m)")
        lora_raw = prod_sb[:, 0, 0, :].rearrange("p (t e r) -> p t e r", t=FT, e=E)
        s_rep = tg[:].rearrange("p b n -> p (b n)")[:, 0:KT * B * P].rearrange("p (k b m) -> p k b m", k=KT, b=B)

        def bank(name):
            return ctx.enter_context(nc.psum_tensor(name, [P, 512], F32))

        ring = [bank(f"ring{i}") for i in range(4)]
        pa = [bank("pa0"), bank("pa1")]
        prod = ctx.enter_context(nc.psum_tensor("prod", [P, NT, 2, P], F32))
        pb = [prod[:, 2 * b:2 * b + 2].rearrange("p c k m -> p (c k m)") for b in range(2)]
        qk_bank = [pa[0], pa[1], ring[2], ring[3]]
        z_bank = [ring[0], ring[3], ring[1], ring[2]]
        score_bank = lambda q, a: (pa if q else pb)[a]
        proj_bank = lambda tile: pb[tile % 2] if tile < 2 * TILES else ring[tile % 4]

        ld_cond, ld_x, ld_const = sig("ld_cond"), sig("ld_x"), sig("ld_const")
        ld_mod, ld_attn, ld_late, ld_low = sig("ld_mod"), sig("ld_attn"), sig("ld_late"), sig("ld_low")
        om_parts, om_moved = sig("om_parts"), sig("om_moved")
        set_const, set_silu, set_wa, set_mod, set_gate = (sig("set_" + x) for x in ("const", "silu", "wa", "mod", "gate"))
        set_act, mods_ps, gates_ps, set_pool = sig("set_act"), sig("mods_ps"), sig("gates_ps"), sig("set_pool")
        wp_done = sig("wp_done")
        late_pe, late_vec, late_act = sig("late_pe"), sig("late_vec"), sig("late_act")
        x_loaded, tok_free = sig("x_loaded", 16), sig("tok_free", 1)
        ln1_vec, ln1_pool, hn_ready = sig("ln1_vec", 8), sig("ln1_pool", 4), sig("hn_ready", 4)
        hT_ps, hT_r, hT_parts = sig("hT_ps", 2), sig("hT_r", 4), sig("hT_parts", 2)
        qk_ps, qk_full, sq_ready = sig("qk_ps", 4), sig("qk_full", 4), sig("sq_ready", 4)
        qk_split = sig("qk_split", 4)
        norm_mm, norm_full, norm_split = sig("norm_mm", 1), sig("norm_full", 1), sig("norm_split", 1)
        qk_out = [sig("q_out", 2 * 16), sig("k_out", 2 * 16)]
        norm_out, moved = sig("norm_out", 2 * 16), sig("moved", 10 * 16)
        v_ps, v_done = sig("v_ps", 2), sig("v_done", 2)
        proj_ps, exp_done = sig("proj_ps", PAIRS * TILES), sig("exp_done", PAIRS * TILES)
        a_ps, am_done = sig("a_ps", H), sig("am_done", H)
        prod_ps, d_ps = sig("prod_ps", GROUPS), sig("d_ps", GROUPS)
        copied = [sig("copied0", GROUPS), sig("copied1", GROUPS)]
        s_step, read_ps = sig("s_step", (NT + 1) * GROUPS), sig("read_ps", GROUPS)
        oT_added, o_ps, y_step = sig("oT_added", GROUPS), sig("o_ps", GROUPS), sig("y_step", 3 * GROUPS)
        mod2_set, mod1_set, mod2c_set = sig("mod2_set", 1), sig("mod1_set", 1), sig("mod2c_set", 1)
        yT_ps, yT_done, prj_ps = sig("yT_ps", 2), sig("yT_done", 2), sig("prj_ps", 2)
        xr_loaded, xr_biased, x2_step = sig("xr_loaded", 16), sig("xr_biased", 1), sig("x2_step", 2)
        ln2_vec, ln2_pool = sig("ln2_vec", 8), sig("ln2_pool", 4)
        h2n_ready = [sig("h2n_vec", 2), sig("h2n_act", 2)]
        h2_ps = sig("h2_ps", 2)
        h2_full, h2_r, h2_parts = [sig("h2_full0", 1), sig("h2_full1", 1)], sig("h2_r", 2), sig("h2_parts", 2)
        lg_ps, lg_done, lt_ps = sig("lg_ps", 1), sig("lg_done", 1), sig("lt_ps", 1)
        low_split, low_masked = sig("low_split", 2), sig("low_masked", 2)
        rt, rt_exp, mask_ps = sig("rt", 24), sig("rt_exp", 1), sig("mask_ps", 2)
        rho_ps, rho_done = sig("rho_ps", 1), sig("rho_done", 1)
        z1_ps, r1_done, z2_ps = sig("z1_ps", FT), sig("r1_done", FT), sig("z2_ps", FT)
        g_step, wo_mm, fin = sig("g_step", 2 * FT), sig("wo_mm", FT), sig("fin", 2)
        scaled = sig("scaled", NT)
        out_done = sig("out_done", 32)

        x_rows = x.rearrange("b (n t p) c -> (b n) p t c", p=P, t=NT)
        out_rows = out.rearrange("b (n t p) c -> (b n) p t c", p=P, t=NT)

        def block_rows(rows, n):
            return rows[n] if isinstance(n, int) else rows[bass.ds(n, 1)].rearrange("o p t c -> p (o t) c")

        def over_tiles(row, k):
            return row.rearrange("p (o w) -> p o w", o=1).broadcast_to([P, k, row.shape[1]])

        def last_bc(ap, k):
            return ap.broadcast_to([ap.shape[0], ap.shape[1], k])

        block = ctx.enter_context(nc.Block())

        @block.sync
        def _(sp):
            def move(dst, src):
                return sp.dma_start(dst.bitcast(F32), src.bitcast(F32))

            def load(signal, *pairs):
                for dst, src in pairs:
                    sp.dma_start(dst, src, allow_slow_non_contiguous=True).then_inc(signal.sem, 16)

            row_bc = lambda ap, w: ap.rearrange("(o c) -> o c", o=1).broadcast_to([P, w])
            load(ld_cond, *((cT[:, k, :], cond[:, k * P:(k + 1) * P].rearrange("b p -> p b")) for k in range(KT)))
            load(ld_x, (tok[:], x_rows[0]))
            load(ld_const, (const[:], consts))
            load(ld_mod, (wmod_raw[0], wmod[0:P, :]), (wmod_raw[1], wmod[P:C, :]))
            load(ld_attn, (om_f, omega), (nrow_f, norm_rows),
                 (wa_raw[0], w_attn[0:P, :]), (wa_raw[1], w_attn[P:C, :]),
                 (qk_bias[:], b_attn[0:2 * C].rearrange("(j p) -> p j", p=P)),
                 (v_bias[:], row_bc(b_attn[2 * C:3 * C], C)), (bp_row, row_bc(b_proj, C)),
                 (bg_row[:], row_bc(bg, E)))
            late = [(wi_raw[k].rearrange("p (t d) -> p t d", t=FT // 2),
                     wi.rearrange("(k t p) d -> k p t d", k=2, p=P)[k]) for k in range(2)]
            late += [(wo_raw[k], wo[k * P:(k + 1) * P, :]) for k in range(KT)]
            late += [(wp, w_proj.rearrange("(k p) n -> p k n", p=P))]
            late += [(lora_raw[:, :, e, :], lora_b[e].rearrange("(t p) r -> p t r", p=P)) for e in range(E)]
            assert len(late) == LATE_LOADS
            for dst, src in late:
                sp.dma_start(dst, src).then_inc(ld_late.sem, 16)
            sp.dma_start(xr[:], x_rows[0]).then_inc(xr_loaded.sem, 16)
            sp.wait_ge(set_pool.sem, 1)
            a_rows = lora_a.rearrange("e r d -> (e r) d")
            for q in range(3):
                sp.dma_start(low_raw[32 * q:32 * q + LORA, :], a_rows).then_inc(ld_low.sem, 16)
            sp.dma_start(low_raw[LOGIT_ROW:LOGIT_ROW + E, :], wg).then_inc(ld_low.sem, 16)
            sp.wait_ge(om_parts.sem, 4)
            for a in range(2):
                for k, part in enumerate((om_r, om_l, om_r)):
                    row = k * PAIR_ROWS + a * DH
                    move(omega_x[row:row + DH, a * M:(a + 1) * M], part[:]).then_inc(om_moved.sem, 16)
            move(omega_x[3 * PAIR_ROWS:XROWS, :], nrow_r[:]).then_inc(om_moved.sem, 16)
            sp.sem_inc(out_done.sem, out_done.per)
            sp.sem_inc(scaled.sem, scaled.per)

            def front_moves(n):
                def out(kind):
                    tiles = slice(2 * kind, 2 * kind + 2)
                    wait(sp, qk_split, n, 2 * kind + 2)
                    for part, src in enumerate((qk_r, qk_l)):
                        sp.dma_start(parts_out[part, tiles].rearrange("j p t -> p j t"),
                                     src[:, tiles, :].bitcast(F32)).then_inc(qk_out[kind].sem, 16)

                def back(kind):
                    wait(sp, qk_out[kind], n, 32)
                    for k, part in enumerate((0, 0, 1)):
                        src = parts_out[part, 2 * kind:2 * kind + 2].rearrange("j (i r) t -> r (j i) t", r=PAIR_ROWS)
                        sp.dma_start(xq[k * PAIR_ROWS:(k + 1) * PAIR_ROWS, kind].bitcast(F32),
                                     src).then_inc(moved.sem, 16)

                out(0)
                back(0)
                out(1)
                wait(sp, norm_split, n, 1)
                for part, src in enumerate((norm_r, norm_l)):
                    sp.dma_start(norms_out[part], src[:].bitcast(F32)).then_inc(norm_out.sem, 16)
                back(1)
                wait(sp, norm_out, n, 32)
                for part in range(2):
                    row = 3 * PAIR_ROWS + 2 * part
                    for a in range(2):
                        src = norms_out[part].rearrange("(j r) t -> r j t", r=VA)[a * GROUP:(a + 1) * GROUP]
                        sp.dma_start(xq[row + a:row + a + 1].rearrange("o k (f i) t -> o (k f) i t", f=2).bitcast(F32),
                                     src.rearrange("i j t -> j i t").rearrange("(o j) i t -> o j i t", o=1))\
                            .then_inc(moved.sem, 16)

            def ffn_stores(n):
                dst = block_rows(out_rows, n)
                for b in range(2):
                    wait(sp, fin, n, b + 1)
                    sp.dma_start(dst[:, 2 * b:2 * b + 2, :],
                                 tg[:, b, :].rearrange("p (t c) -> p t c", t=2)).then_inc(out_done.sem, 16)

            front_moves(0)
            with sp.Fori(0, NB - 1) as i:
                wait(sp, tok_free, i, 1)
                sp.dma_start(tok[:], block_rows(x_rows, i + 1)).then_inc(x_loaded.sem, 16)
                front_moves(i + 1)
                ffn_stores(i)
                sp.dma_start(xr[:], block_rows(x_rows, i + 1)).then_inc(xr_loaded.sem, 16)
            ffn_stores(NB - 1)
            wait(sp, out_done, NB, out_done.per)

        @block.tensor
        def _(pe):
            def split3(dst, w_r, w_l, v_r, v_l, first, last):
                pe.matmul(dst, w_r, v_r, start=first, stop=False)
                pe.matmul(dst, w_l, v_r, start=False, stop=False)
                return pe.matmul(dst, w_r, v_l, start=False, stop=last)

            def setup_mods():
                pe.wait_ge(ld_mod.sem, 16 * KT)
                pe.wait_ge(set_silu.sem, 4)
                for m, which in enumerate((1, 0, 4, 3)):
                    for half in range(KT):
                        col = (m * KT + half) * B
                        for k in range(KT):
                            mm = pe.matmul(pa[0][:, col:col + B],
                                      wmod_raw[k][:, which * C + half * P:which * C + half * P + P],
                                      sT[:, k, :], start=k == 0, stop=k == KT - 1)
                mm.then_inc(mods_ps.sem, 1)
                for which, dst in ((2, pb[0]), (5, pb[1])):
                    for b in range(B):
                        for k in range(KT):
                            mm = pe.matmul(dst[:, b * C:(b + 1) * C], s_rep[:, k, b, :],
                                           wmod_raw[k][:, which * C:(which + 1) * C],
                                           start=k == 0, stop=k == KT - 1)
                mm.then_inc(gates_ps.sem, 1)

            def transpose1(n):
                wait(pe, hn_ready, n, NT)
                for k in range(KT):
                    for t in range(NT):
                        mm = pe.transpose(ring[k][:, t * P:(t + 1) * P], tok[:, t, k * P:(k + 1) * P], ident)
                    mm.then_inc(hT_ps.sem, 1)

            def qk(n, j, ks=range(KT)):
                if j == 0:
                    wait(pe, hT_parts, n, 2)
                for k in ks:
                    w = slice(j * P, (j + 1) * P)
                    mm = split3(qk_bank[j][:], wa_r[:, k, w], wa_l[:, k, w], h_r[:, k, :], h_l[:, k, :],
                                k == 0, k == KT - 1)
                if KT - 1 in ks:
                    mm.then_inc(qk_ps.sem, 1)

            def norms(n):
                wait(pe, sq_ready, n, 4)
                for j in range(4):
                    mm = pe.matmul(ring[0][j * VA:(j + 1) * VA, :], headsum, qk_sq[:, j, :], start=True, stop=True)
                mm.then_inc(norm_mm.sem, 1)

            def values(n):
                for t in range(NT):
                    dst = pb[t // 2][:, t % 2 * C:(t % 2 + 1) * C]
                    tt = slice(t * P, (t + 1) * P)
                    for k in range(KT):
                        mm = split3(dst, h_r[:, k, tt], h_l[:, k, tt],
                                    wa_r[:, k, 2 * C:3 * C], wa_l[:, k, 2 * C:3 * C], k == 0, k == KT - 1)
                    if t % 2:
                        mm.then_inc(v_ps.sem, 1)

            def setup_late():
                pe.wait_ge(ld_late.sem, 16 * LATE_LOADS)
                wait(pe, v_done, 0, 2)
                wait(pe, norm_split, 0, 1)
                for k in range(KT):
                    for half in range(2):
                        for t in range(4):
                            mm = pe.transpose(ring[2 * k + half][:, t * P:(t + 1) * P],
                                              wi_raw[half][:, t * C + k * P:t * C + (k + 1) * P], ident)
                        mm.then_inc(late_pe.sem, 1)
                for q in range(4):
                    for t in range(2):
                        for k in range(KT):
                            f = (2 * q + t) * P
                            mm = pe.transpose((*pa, *pb)[q][:, (t * KT + k) * P:(t * KT + k + 1) * P],
                                              wo_raw[k][:, f:f + P], ident)
                    mm.then_inc(late_pe.sem, 1)
                pe.wait_ge(ld_low.sem, 16 * 4)
                pe.wait_ge(late_vec.sem, 2)
                for k in range(KT):
                    mm = pe.transpose(ring[0][:, k * P:(k + 1) * P], low_raw[:, k * P:(k + 1) * P], ident)
                mm.then_inc(late_pe.sem, 1)
                pe.wait_ge(set_pool.sem, 9)
                pe.wait_ge(late_vec.sem, 6)
                for half, src in enumerate((mk1, mk2)):
                    for t in range(4):
                        mm = pe.transpose(ring[1 + half][0:LROWS, t * P:(t + 1) * P], src[:, t, :], ident)
                    mm.then_inc(late_pe.sem, 1)
                pe.wait_ge(late_vec.sem, 12)
                pe.wait_ge(late_act.sem, 5)
                pe.wait_ge(wp_done.sem, B)

            def features(n, p, tiles=range(TILES)):
                for k in tiles:
                    tile = p * TILES + k
                    dst = proj_bank(tile)
                    if tile == 0:
                        wait(pe, moved, n, moved.per)
                    if 2 <= tile < 2 * TILES:
                        wait(pe, exp_done, n, tile - 1)
                    if tile >= 2 * TILES + 4:
                        wait(pe, exp_done, n, tile - 3)
                    if k < 4:
                        mm = pe.matmul(dst[:], omega_x[:, k // 2 * M:(k // 2 + 1) * M], xq[:, k % 2, p, :],
                                       start=True, stop=True)
                    else:
                        for c in range(2):
                            t = (2 * (k - 4) + c) * P
                            mm = pe.matmul(dst[:, c * 2 * M:(c + 1) * 2 * M], xq[:, 1, p, t:t + P], omega_x[:],
                                           start=True, stop=True)
                    mm.then_inc(proj_ps.sem, 1)

            def scores(n, q, a):
                if q:
                    wait(pe, exp_done, n, q * TILES + 2 * a + 2)
                if q == 0:
                    wait(pe, exp_done, n, 2 * TILES)
                if q == 1:
                    wait(pe, scaled, n, 2 * a + 2)
                if q > 1:
                    wait(pe, am_done, n, 2 * (q - 1) + a + 1)
                for c in range(NT):
                    tt = slice(c * P, (c + 1) * P)
                    mm = pe.matmul(score_bank(q, a)[:, tt], phkT[:, q % 2, a, tt], phq[:, q // 2 % 2, 2 * (q % 2) + a, tt],
                                   start=True, stop=True)
                mm.then_inc(a_ps.sem, 1)

            def products(n, gr):
                if gr == 0:
                    wait(pe, v_done, n, 2)
                else:
                    wait(pe, y_step, n, 3 * gr)
                wait(pe, am_done, n, GROUP * (gr + 1))
                wait(pe, exp_done, n, 2 * TILES * (gr + 1))
                for j in range(GROUP):
                    rows = slice(j * VA, (j + 1) * VA)
                    for c in range(NT):
                        both = am_phk[:, 0:2 + gr % 2:1 + gr % 2, j, c * P:(c + 1) * P]
                        mm = pe.matmul(prod[rows, c], v_ones[:, c, GROUP * gr + j, :], both, start=True, stop=True)
                mm.then_inc(prod_ps.sem, 1)

            def state_transpose(n, gr):
                for c in range(NT):
                    if c % 2 == 0:
                        wait(pe, copied[c // 2], n, gr + 1)
                    mm = pe.transpose(prod[:, c, 1, :], prod_sb[:, c, 1, :], ident)
                mm.then_inc(d_ps.sem, 1)

            def state_reads(n, gr):
                wait(pe, s_step, n, (NT + 1) * (gr + 1))
                for j in range(GROUP):
                    rows = slice(j * VA, (j + 1) * VA)
                    for c in range(NT):
                        mm = pe.matmul(prod[rows, c, 1, :], s_sb[:, c, rows], phq[:, gr % 2, j, c * P:(c + 1) * P],
                                       start=True, stop=True)
                mm.then_inc(read_ps.sem, 1)

            def out_transpose(n, gr):
                wait(pe, oT_added, n, gr + 1)
                for c in range(NT):
                    mm = pe.transpose(prod[:, c, 0, :], oT_sb[:, c, :], ident)
                mm.then_inc(o_ps.sem, 1)

            def attend(n, front_next):
                scores(n, 0, 0)
                scores(n, 0, 1)
                features(n, 2, range(4))
                scores(n, 1, 0)
                features(n, 2, range(4, TILES))
                scores(n, 1, 1)
                features(n, 3, range(4))
                for gr in range(GROUPS):
                    more = gr + 1 < GROUPS
                    q = 2 * gr + 2
                    products(n, gr)
                    if q + 1 < PAIRS:
                        features(n, q + 1, range(4, TILES))
                    if more:
                        scores(n, q, 0)
                    elif front_next:
                        qk(n + 1, 0)
                    state_transpose(n, gr)
                    if more:
                        scores(n, q, 1)
                        scores(n, q + 1, 0)
                    elif front_next:
                        qk(n + 1, 1)
                    state_reads(n, gr)
                    if q + 2 < PAIRS:
                        features(n, q + 2, range(4))
                    elif more:
                        scores(n, q + 1, 1)
                    elif front_next:
                        qk(n + 1, 2, [0])
                    out_transpose(n, gr)
                    if q + 2 < PAIRS:
                        features(n, q + 2, range(4, TILES))
                        scores(n, q + 1, 1)
                        features(n, q + 3, range(4))
                    elif more and front_next:
                        wait(pe, exp_done, n, PAIRS * TILES)
                        transpose1(n + 1)

            def y_transpose(n):
                wait(pe, y_step, n, 3 * GROUPS)
                for k in range(KT):
                    for t in range(NT):
                        mm = pe.transpose(ring[k][:, t * P:(t + 1) * P], y[:, t, k * P:(k + 1) * P], ident)
                    mm.then_inc(yT_ps.sem, 1)

            def projection(n, front_next):
                wait(pe, yT_done, n, KT)
                if front_next:
                    wait(pe, qk_split, n + 1, 2)
                row = n // BLOCKS_PER_ROW
                for t in range(NT):
                    dst = pa[t // 2][:, t % 2 * C:(t % 2 + 1) * C]
                    for k in range(KT):
                        w = wp_ga[:, row, k, :] if isinstance(n, int) else \
                            wp_ga[:, bass.ds(row, 1), k, :].rearrange("p o c -> p (o c)")
                        mm = pe.matmul(dst, yT[:, k, t * P:(t + 1) * P], w, start=k == 0, stop=k == KT - 1)
                    if t % 2:
                        mm.then_inc(prj_ps.sem, 1)

            def base(n, f, ks=range(KT)):
                if f == 0:
                    wait(pe, h2_parts, n, 2)
                if f >= 4:
                    wait(pe, g_step, n, 2 * (f - 4) + 1)
                w = slice(f * P, (f + 1) * P)
                for k in ks:
                    split3(z_bank[f % 4][:], wi_r[:, k, w], wi_l[:, k, w], h_r[:, k, :], h_l[:, k, :], k == 0, False)

            def ffn_head(n, front_next):
                for t in range(NT):
                    wait(pe, h2n_ready[t // 2], n, t % 2 + 1)
                    for k, dst in enumerate((ring[3], ring[1])):
                        mm = pe.transpose(dst[:, t * P:(t + 1) * P], tok[:, t, k * P:(k + 1) * P], ident)
                        if t == NT - 1:
                            mm.then_inc(h2_ps.sem, 1)
                for k in range(KT):
                    wait(pe, h2_full[k], n, 1)
                    mm = pe.matmul(ring[2][:], low_t[:, k, :], h_f[:, k, :], start=k == 0, stop=k == KT - 1)
                    if k == 0:
                        mm.then_inc(tok_free.sem, 1)
                mm.then_inc(lg_ps.sem, 1)
                if front_next:
                    wait(pe, norm_split, n + 1, 1)
                base(n, 0, [0])
                wait(pe, lg_done, n, 1)
                base(n, 0, [1])
                rows = slice(LOGIT_ROW, LOGIT_ROW + E)
                for t in range(NT):
                    mm = pe.transpose(pa[0][:, t * E:(t + 1) * E], lg[rows, t * P:(t + 1) * P], ident[rows, rows])
                mm.then_inc(lt_ps.sem, 1)
                for f in range(1, 4):
                    base(n, f)

            def masks(n):
                for src, need, dst in ((mk1, 18, pa[1]), (mk2, 21, pa[0])):
                    wait(pe, rt, n, need)
                    for t in range(NT):
                        mm = pe.transpose(dst[0:LROWS, t * P:(t + 1) * P], src[:, t, :], ident)
                    mm.then_inc(mask_ps.sem, 1)

            def ratio(n):
                for t in range(NT):
                    mm = pe.transpose(pa[1][:, t * P:(t + 1) * P], r2[:, 0, t * P:(t + 1) * P], ident)
                mm.then_inc(rho_ps.sem, 1)

            def experts(n, front_next):
                tile = 0
                for f in range(FT + 3):
                    if f < FT:
                        if f == 0:
                            wait(pe, low_masked, n, 1)
                        w = slice(f * P, (f + 1) * P)
                        pe.matmul(z_bank[f % 4][:], lora_w[:, w], low1, start=False,
                                  stop=True).then_inc(z1_ps.sem, 1)
                    if f == 0:
                        wait(pe, rt, n, 22)
                        ratio(n)
                    if 4 <= f + 2 < FT:
                        base(n, f + 2)
                    if 1 <= f <= FT:
                        if f == 1:
                            wait(pe, low_masked, n, 2)
                        wait(pe, r1_done, n, f)
                        w = slice((f - 1) * P, f * P)
                        pe.matmul(z_bank[(f - 1) % 4][:], lora_w[:, w], low2, start=False, stop=True,
                                  skip_group_check=True).then_inc(z2_ps.sem, 1)
                    if front_next:
                        if f == 1:
                            wait(pe, v_done, n + 1, 2)
                        for _ in range(AHEAD.get(f, 0)):
                            features(n + 1, tile // TILES, [tile % TILES])
                            tile += 1
                    if f >= 3:
                        k = f - 3
                        if k == 0:
                            wait(pe, rho_done, n, 1)
                        wait(pe, g_step, n, 2 * k + 2)
                        for t in range(NT):
                            mm = pe.matmul(pa[t // 2][:, t % 2 * C:(t % 2 + 1) * C], g[:, k % 4, t * P:(t + 1) * P],
                                           wo_t[:, k, :], start=k == 0 and t % 2 == 0, stop=k == FT - 1,
                                           skip_group_check=True)
                        mm.then_inc(wo_mm.sem, 1)

            pe.wait_ge(ld_const.sem, 16)
            transpose1(0)
            setup_mods()
            pe.wait_ge(set_wa.sem, 4 * KT)
            pe.wait_ge(set_mod.sem, 4)
            for j in range(4):
                qk(0, j)
            norms(0)
            pe.wait_ge(set_gate.sem, 11)
            values(0)
            setup_late()
            pe.wait_ge(om_moved.sem, 16 * 7)
            pe.nop().then_inc(tok_free.sem, 1)
            features(0, 0)
            features(0, 1)

            def after_attend(n, front_next):
                if front_next:
                    qk(n + 1, 2, [1])
                y_transpose(n)
                if front_next:
                    qk(n + 1, 3)
                projection(n, front_next)
                if front_next:
                    norms(n + 1)
                    values(n + 1)
                ffn_head(n, front_next)
                masks(n)
                experts(n, front_next)

            with pe.Fori(0, NB - 1) as i:
                attend(i, True)
                after_attend(i, True)
            attend(NB - 1, False)
            after_attend(NB - 1, False)

        @block.scalar
        def _(act):
            def setup():
                act.wait_ge(ld_cond.sem, 16 * KT)
                act.activation(sT[:], cT[:], ACT.Exp, scale=-1.0).then_inc(set_act.sem, 1)
                act.wait_ge(ld_attn.sem, 16 * ATTN_LOADS)
                act.activation(qk_bias[:], qk_bias[:], ACT.Copy, scale=Q_SCALE).then_inc(set_act.sem, 1)

            def front_hT(n):
                wait(act, mod1_set, n, 1)
                for k in range(KT):
                    wait(act, hT_ps, n, k + 1)
                    for dst in (h_f, h_r):
                        act.activation(dst[:, k, :], ring[k][:], ACT.Identity, bias=mod1_now[:, KT + k:KT + k + 1],
                                       scale=mod1_now[:, k:k + 1]).then_inc(hT_r.sem, 1)

            def front_qk(n, j):
                wait(act, qk_ps, n, j + 1)
                act.activation(qk_r[:, j, :], qk_bank[j][:], ACT.Identity,
                               bias=qk_bias[:, j:j + 1]).then_inc(qk_full.sem, 1)
                act.activation(qk_sq[:, j, :], qk_bank[j][:], ACT.Square,
                               bias=qk_bias[:, j:j + 1]).then_inc(sq_ready.sem, 1)

            def front_norm(n):
                wait(act, norm_mm, n, 1)
                act.activation(norm_r[:], ring[0][:], ACT.Copy).then_inc(norm_full.sem, 1)

            def setup_late():
                for q in range(4):
                    act.wait_ge(late_pe.sem, 5 + q)
                    act.activation(wo_t[:, 2 * q:2 * q + 2, :].rearrange("p t c -> p (t c)"), (*pa, *pb)[q][:],
                                   ACT.Copy).then_inc(late_act.sem, 1)
                act.wait_ge(late_pe.sem, 9)
                act.activation(low_t[:].rearrange("p k m -> p (k m)"), ring[0][:, 0:KT * P],
                               ACT.Copy).then_inc(late_act.sem, 1)

            def features(n, q, tiles):
                for k in tiles:
                    tile = q * TILES + k
                    wait(act, proj_ps, n, tile + 1)
                    slot = q // 2 % 2
                    if k >= 4:
                        c = 2 * (k - 4) * P
                        dst = am_phk[:, 1 + slot, 2 * (q % 2):2 * (q % 2) + 2, c:c + 2 * P]\
                            .rearrange("p a (c m) -> p c a m", c=2)
                        src = proj_bank(tile)[:].rearrange("p (c a m) -> p c a m", c=2, a=2)
                    else:
                        dst = (phq[:, slot, 2 * (q % 2) + k // 2, :], phkT[:, q % 2, k // 2, :])[k % 2]
                        src = proj_bank(tile)[:]
                    act.activation(dst, src, ACT.Exp).then_inc(exp_done.sem, 1)

            def attend(n, front_next):
                features(n, 2, range(TILES))
                for gr in range(GROUPS):
                    ahead = 2 * gr + 3
                    if ahead < PAIRS:
                        features(n, ahead, range(4))
                    wait(act, prod_ps, n, gr + 1)
                    act.activation(prod_sb[:, 0:2].rearrange("p c k m -> p (c k m)"), pb[0],
                                   ACT.Copy).then_inc(copied[0].sem, 1)
                    if ahead < PAIRS:
                        features(n, ahead, range(4, TILES))
                    if ahead + 1 < PAIRS:
                        features(n, ahead + 1, range(TILES))
                    if front_next and gr == GROUPS - 2:
                        front_hT(n + 1)

            def y_copy(n):
                for k in range(KT):
                    wait(act, yT_ps, n, k + 1)
                    act.activation(yT[:, k, :], ring[k][:], ACT.Copy).then_inc(yT_done.sem, 1)

            def ffn(n, front_next):
                wait(act, ln2_pool, n, 4)
                for t in range(2, NT):
                    act.activation(tok[:, t, :], xr[:, t, :], ACT.Identity, bias=shift[:, t:t + 1],
                                   scale=rstd[:, t:t + 1]).then_inc(h2n_ready[1].sem, 1)
                wait(act, mod2c_set, n, 1)
                wait(act, h2_ps, n, 1)
                act.activation(h_f[:, 0, :], ring[3][:], ACT.Identity, bias=mod2_cols[:, KT:KT + 1],
                               scale=mod2_cols[:, 0:1]).then_inc(h2_full[0].sem, 1)
                for k in range(KT):
                    wait(act, h2_full[k], n, 1)
                    act.activation(h_r[:, k, :], h_f[:, k, :], ACT.Copy).then_inc(h2_r.sem, 1)
                wait(act, lg_ps, n, 1)
                act.activation(lg, ring[2][:], ACT.Copy).then_inc(lg_done.sem, 1)
                wait(act, rt, n, 10)
                act.activation(exo[:], ex[:], ACT.Exp).then_inc(rt_exp.sem, 1)
                tile = 0
                for f in range(FT + 3):
                    if f < FT:
                        wait(act, z1_ps, n, f + 1)
                        if f >= 4:
                            wait(act, wo_mm, n, f - 3)
                        act.activation(g[:, f % 4, :], z_bank[f % 4][:], ACT.Relu).then_inc(r1_done.sem, 1)
                    if f == 0:
                        wait(act, rho_ps, n, 1)
                        act.activation(rho, pa[1][:], ACT.Copy).then_inc(rho_done.sem, 1)
                    for _ in range(AHEAD.get(f, 0) if front_next else 0):
                        features(n + 1, tile // TILES, [tile % TILES])
                        tile += 1

            setup()
            act.wait_ge(set_act.sem, 2)
            front_hT(0)
            for j in range(4):
                front_qk(0, j)
            front_norm(0)
            setup_late()
            features(0, 0, range(TILES))
            features(0, 1, range(TILES))

            def after_attend(n, front_next):
                if front_next:
                    front_qk(n + 1, 0)
                    front_qk(n + 1, 1)
                y_copy(n)
                if front_next:
                    front_qk(n + 1, 2)
                    front_qk(n + 1, 3)
                    front_norm(n + 1)
                ffn(n, front_next)

            with act.Fori(0, NB - 1) as i:
                attend(i, True)
                after_attend(i, True)
            attend(NB - 1, False)
            after_attend(NB - 1, False)

        @block.vector
        def _(dve):
            def chain(signal):
                count = [0]

                def step(ins):
                    count[0] += 1
                    ins.then_inc(signal.sem, 1)
                    dve.wait_ge(signal.sem, count[0])
                return step

            def setup_constants():
                for tile, value in ((neg_half[:], -0.5), (neg_one[:], -1.0), (eps[:], EPS_LN), (state[:], 0.0),
                                    (v_ones[:, :, :, DH:VA], 1.0)):
                    dve.memset(tile, value).then_inc(set_const.sem, 1)
                dve.memset(omega_x[:].bitcast(F32), 0.0).then_inc(om_parts.sem, 1)

            def setup_silu():
                step = chain(set_silu)
                c_col, s_col = (ap[:].rearrange("p k b -> p (k b)") for ap in (cT, sT))
                dve.wait_ge(set_act.sem, 1)
                step(dve.tensor_scalar(ex[:, 0, 0:KT * B], s_col, 1.0, None, ALU.add))
                step(dve.reciprocal(exo[:, 0, 0:KT * B], ex[:, 0, 0:KT * B]))
                step(dve.tensor_tensor(s_col, c_col, exo[:, 0, 0:KT * B], ALU.mult))
                step(dve.tensor_copy(s_rep.rearrange("p k b m -> p (k b) m"),
                                     last_bc(sT[:].rearrange("p k (b o) -> p (k b) o", o=1), P)))

            def setup_attention():
                dve.wait_ge(ld_attn.sem, 16 * ATTN_LOADS)
                dve.tensor_copy(om_r[:], om_f).then_inc(om_parts.sem, 1)
                dve.tensor_copy(nrow_r[:], nrow_f).then_inc(om_parts.sem, 1)
                qk, v = slice(0, 2 * C), slice(2 * C, 3 * C)
                for k in range(KT):
                    dve.tensor_scalar(wa_r[:, k, qk], wa_raw[k][:, qk], Q_SCALE, None, ALU.mult).then_inc(set_wa.sem, 1)
                    dve.tensor_copy(wa_r[:, k, v], wa_raw[k][:, v]).then_inc(set_wa.sem, 1)
                dve.wait_ge(om_parts.sem, 2)
                dve.tensor_tensor(om_l[:], om_f, om_r[:].bitcast(F32), ALU.subtract).then_inc(om_parts.sem, 1)
                dve.wait_ge(set_wa.sem, 2 * KT)
                for k in range(KT):
                    dve.scalar_tensor_tensor(wa_l[:, k, qk], wa_raw[k][:, qk], Q_SCALE, wa_r[:, k, qk].bitcast(F32),
                                             ALU.mult, ALU.subtract).then_inc(set_wa.sem, 1)
                    dve.tensor_tensor(wa_l[:, k, v], wa_raw[k][:, v], wa_r[:, k, v].bitcast(F32),
                                      ALU.subtract).then_inc(set_wa.sem, 1)

            def setup_mods():
                step = chain(set_mod)
                dve.wait_ge(mods_ps.sem, 1)
                mods = pa[0][:, 0:8 * B].rearrange("p (m b) -> p b m", b=B)
                step(dve.tensor_scalar(mod1[:, :, 0:KT], mods[:, :, 0:2], 1.0, None, ALU.add))
                step(dve.tensor_copy(mod1[:, :, KT:2 * KT], mods[:, :, 2:4]))
                dve.tensor_copy(mod1_now[:], mod1[:, 0, :]).then_inc(mod1_set.sem, 1)
                step(dve.tensor_scalar(mod2[:, :, 2 * C:2 * C + KT], mods[:, :, 4:6], 1.0, None, ALU.add))
                step(dve.tensor_copy(mod2[:, :, 2 * C + KT:2 * C + 2 * KT], mods[:, :, 6:8]))

            def setup_gates():
                step = chain(set_gate)
                dve.wait_ge(gates_ps.sem, 1)
                for q, src in enumerate(pb):
                    rows = src.rearrange("p (b c) -> p b c", b=B)
                    gate = (ga_rows, mod2[:, :, 0:C])[q]
                    tmp = y[:, 0:2, :]
                    step(dve.tensor_copy(tmp, rows))
                    step(dve.scalar_tensor_tensor(gate, tmp, -1.0, tmp, ALU.mult, ALU.max))
                    step(dve.tensor_scalar(gate, gate, 0.25, None, ALU.max))
                    step(dve.tensor_scalar(tmp, tmp, 0.0, 2.0, ALU.is_ge, ALU.mult))
                    step(dve.scalar_tensor_tensor(gate, tmp, -1.0, gate, ALU.add, ALU.mult))
                step(dve.tensor_tensor(mod2[:, :, C:2 * C], ga_rows, over_tiles(bp_row, B), ALU.mult))

            def row_of(mod, n):
                row = n // BLOCKS_PER_ROW
                return mod[:, row, :] if isinstance(n, int) else \
                    mod[:, bass.ds(row, 1), :].rearrange("p o c -> p (o c)")

            def normalize_apply(n, src, pool, ready):
                wait(dve, pool, n, 3)
                for t in range(NT if src is tok else 2):
                    dve.tensor_scalar(tok[:, t, :], src[:, t, :], mv[:, t, 0:1], rstd[:, t:t + 1],
                                      ALU.subtract, ALU.mult).then_inc(ready.sem, 1)

            def ln1_stats(n, first):
                if first:
                    dve.wait_ge(ld_x.sem, 16)
                else:
                    wait(dve, x_loaded, n - 1, 16)
                for t in range(NT):
                    dve.bn_stats(stats[:, t, :], tok[:, t, :]).then_inc(ln1_vec.sem, 1)
                wait(dve, ln1_vec, n, NT)
                if not first:
                    dve.tensor_copy(mod1_now[:], row_of(mod1, n)).then_inc(mod1_set.sem, 1)
                for t in range(NT):
                    dve.bn_aggr(mv[:, t, :], stats[:, t, :]).then_inc(ln1_vec.sem, 1)

            def h2_copy(n):
                wait(dve, h2_ps, n, 2)
                dve.tensor_scalar(h_f[:, 1, :], ring[1][:], mod2_cols[:, 1:2], mod2_cols[:, KT + 1:KT + 2],
                                  ALU.mult, ALU.add).then_inc(h2_full[1].sem, 1)

            def split_h(n, rounded, per, parts):
                for k in range(KT):
                    wait(dve, rounded, n, per * (k + 1))
                    dve.tensor_tensor(h_l[:, k, :], h_f[:, k, :], h_r[:, k, :].bitcast(F32),
                                      ALU.subtract).then_inc(parts.sem, 1)

            def split_qk(n, j):
                wait(dve, sq_ready, n, j + 1)
                dve.scalar_tensor_tensor(qk_l[:, j, :], qk_bank[j][:], qk_bias[:, j:j + 1],
                                         qk_r[:, j, :].bitcast(F32), ALU.add, ALU.subtract).then_inc(qk_split.sem, 1)

            def split_norm(n):
                wait(dve, norm_full, n, 1)
                dve.tensor_tensor(norm_l[:], ring[0][:], norm_r[:].bitcast(F32),
                                  ALU.subtract).then_inc(norm_split.sem, 1)

            def values(n):
                for b in range(2):
                    wait(dve, v_ps, n, b + 1)
                    dve.tensor_tensor(v_ones[:, 2 * b:2 * b + 2, :, 0:DH],
                                      pb[b].rearrange("p (t h d) -> p t h d", t=2, d=DH),
                                      over_tiles(v_bias[:], 2).rearrange("p t (h d) -> p t h d", d=DH),
                                      ALU.add).then_inc(v_done.sem, 1)

            def setup_late():
                dve.wait_ge(ld_late.sem, 16 * LATE_LOADS)
                for row in range(B):
                    dve.tensor_tensor(wp_ga[:, row], wp, over_tiles(ga_rows[:, row], KT),
                                      ALU.mult).then_inc(wp_done.sem, 1)
                for k in range(KT):
                    for half in range(2):
                        q = 2 * k + half
                        dve.wait_ge(late_pe.sem, q + 1)
                        w = slice(half * T, (half + 1) * T)
                        dve.tensor_copy(wi_r[:, k, w], ring[q][:]).then_inc(late_vec.sem, 1)
                        dve.wait_ge(late_vec.sem, 2 * q + 1)
                        dve.tensor_tensor(wi_l[:, k, w], ring[q][:], wi_r[:, k, w].bitcast(F32),
                                          ALU.subtract).then_inc(late_vec.sem, 1)
                for half in range(2):
                    dve.wait_ge(late_pe.sem, 10 + half)
                    w = slice(half * T, (half + 1) * T)
                    dve.tensor_copy(lora_w[:, w], ring[1 + half][0:LROWS, :]).then_inc(late_vec.sem, 1)
                    dve.wait_ge(late_vec.sem, 9 + 2 * half)
                    dve.tensor_tensor(lora_w[32:64, w], ring[1 + half][32:64, :], lora_w[32:64, w].bitcast(F32),
                                      ALU.subtract).then_inc(late_vec.sem, 1)

            def causal_scores(n, q, a):
                wait(dve, a_ps, n, 2 * q + a + 1)
                dve.tensor_tensor(am[:, 2 * (q % 2) + a, :].rearrange("p (c t) -> p c t", c=NT),
                                  score_bank(q, a)[:].rearrange("p (c t) -> p c t", c=NT),
                                  over_tiles(causal, NT), ALU.min).then_inc(am_done.sem, 1)

            def advance_state(n, gr):
                fresh = (n % BLOCKS_PER_ROW + BLOCKS_PER_ROW - 1) // BLOCKS_PER_ROW
                start = state[:, fresh, gr, :] if isinstance(n, int) else \
                    state[:, bass.ds(fresh, 1), gr, :].rearrange("p o m -> p (o m)")
                c0 = (NT + 1) * gr
                wait(dve, d_ps, n, gr + 1)
                dve.tensor_copy(s_sb[:, 0, :], start).then_inc(s_step.sem, 1)
                for c in range(NT):
                    wait(dve, s_step, n, c0 + c + 1)
                    after = s_sb[:, c + 1, :] if c + 1 < NT else state[:, 1, gr, :]
                    dve.tensor_tensor(after, s_sb[:, c, :], prod[:, c, 1, :], ALU.add).then_inc(s_step.sem, 1)

            def add_reads(n, gr):
                wait(dve, read_ps, n, gr + 1)
                dve.tensor_tensor(oT_sb[:], prod_sb[:, :, 0, :], prod[:, :, 1, :], ALU.add).then_inc(oT_added.sem, 1)

            def divide(n, gr):
                wait(dve, o_ps, n, gr + 1)
                o = prod[:, :, 0, :].rearrange("p c (j d) -> p c j d", j=GROUP)
                dve.tensor_scalar(den[:], o[:, :, :, DH], EPS_DEN, None, ALU.add).then_inc(y_step.sem, 1)
                wait(dve, y_step, n, 3 * gr + 1)
                dve.reciprocal(rden[:], den[:]).then_inc(y_step.sem, 1)
                wait(dve, y_step, n, 3 * gr + 2)
                dve.tensor_tensor(y[:, :, gr * GROUP * DH:(gr + 1) * GROUP * DH]
                                  .rearrange("p c (j d) -> p c j d", j=GROUP), o[:, :, :, 0:DH],
                                  rden[:].rearrange("p c (j o) -> p c j o", o=1).broadcast_to([P, NT, GROUP, DH]),
                                  ALU.mult).then_inc(y_step.sem, 1)

            def attend(n, front_next):
                for q in range(2):
                    for a in range(2):
                        causal_scores(n, q, a)
                for gr in range(GROUPS):
                    more = gr + 1 < GROUPS
                    q = 2 * gr + 2
                    wait(dve, prod_ps, n, gr + 1)
                    dve.tensor_copy(prod_sb[:, 2:4].rearrange("p c k m -> p (c k m)"), pb[1])\
                        .then_inc(copied[1].sem, 1)
                    if more:
                        causal_scores(n, q, 0)
                    advance_state(n, gr)
                    if more:
                        causal_scores(n, q, 1)
                        causal_scores(n, q + 1, 0)
                    elif front_next:
                        split_qk(n + 1, 0)
                    add_reads(n, gr)
                    if gr == GROUPS - 2:
                        causal_scores(n, q + 1, 1)
                    divide(n, gr)
                    if gr < GROUPS - 2:
                        causal_scores(n, q + 1, 1)
                    if front_next and gr == 0:
                        ln1_stats(n + 1, False)
                    if front_next and gr == 1:
                        normalize_apply(n + 1, tok, ln1_pool, hn_ready)
                    if front_next and gr == 2:
                        split_h(n + 1, hT_r, 2, hT_parts)

            def residual(n):
                wait(dve, xr_biased, n, 1)
                for b in range(2):
                    wait(dve, prj_ps, n, b + 1)
                    two = xr[:, 2 * b:2 * b + 2, :].rearrange("p t c -> p (t c)")
                    dve.tensor_tensor(two, pa[b][:], two, ALU.add).then_inc(x2_step.sem, 1)
                    wait(dve, x2_step, n, b + 1)
                    for t in (2 * b, 2 * b + 1):
                        dve.bn_stats(stats[:, t, :], xr[:, t, :]).then_inc(ln2_vec.sem, 1)
                wait(dve, ln2_vec, n, NT)
                dve.tensor_copy(mod2_cols[:], row_of(mod2, n)[:, 2 * C:]).then_inc(mod2c_set.sem, 1)
                for t in range(NT):
                    dve.bn_aggr(mv[:, t, :], stats[:, t, :]).then_inc(ln2_vec.sem, 1)

            def router(n):
                count = [0]

                def link(ins):
                    count[0] += 1
                    ins.then_inc(rt.sem, 1)

                def after(c=None):
                    wait(dve, rt, n, c or count[0])

                wait(dve, lt_ps, n, 1)
                logit, eq, pr, one1, rest, one2, diff = (route[:, k] for k in range(7))
                m1, m2, pm = rmax[:, 0], rmax[:, 1], rmax[:, 2]
                col = lambda ap: last_bc(ap.rearrange("p (t o) -> p t o", o=1), E)
                link(dve.tensor_tensor(logit, pa[0][:, 0:NT * E].rearrange("p (t e) -> p t e", e=E),
                                       over_tiles(bg_row[:], NT), ALU.add))
                after()

                def first_of_largest(values, largest, one):
                    link(dve.tensor_tensor(eq, values, col(largest), ALU.is_equal))
                    after()
                    link(dve.tensor_tensor(pr, eq, over_tiles(prio, NT), ALU.mult))
                    after()
                    link(dve.tensor_reduce(pm, pr, AX.X, ALU.max))
                    after()
                    link(dve.tensor_tensor(one, pr, col(pm), ALU.is_equal))
                    after()

                link(dve.tensor_reduce(m1, logit, AX.X, ALU.max))
                after()
                first_of_largest(logit, m1, one1)
                link(dve.scalar_tensor_tensor(rest, one1, PAD, logit, ALU.mult, ALU.add))
                after()
                link(dve.tensor_reduce(m2, rest, AX.X, ALU.max))
                after()
                link(dve.tensor_tensor(ex[:, :, 0:E], logit, col(m1), ALU.subtract))
                link(dve.tensor_tensor(ex[:, :, E], m2, m1, ALU.subtract))
                assert count[0] == 10
                first_of_largest(rest, m2, one2)
                link(dve.tensor_tensor(diff, one2, one1, ALU.subtract))
                after()
                for mk, one in ((mk1, one1), (mk2, diff)):
                    for q in range(3):
                        link(dve.tensor_copy(mk[:, :, 32 * q:32 * q + LORA].rearrange("p t (e r) -> p t e r", r=R),
                                             one.rearrange("p t (e o) -> p t e o", o=1)
                                             .broadcast_to([P, NT, E, R])))
                wait(dve, rt_exp, n, 1)
                dve.tensor_copy(r2[:, 0, :].rearrange("p (t m) -> p t m", t=NT), last_bc(exo[:, :, E:E + 1], P))\
                   .then_inc(rt.sem, 1)
                dve.tensor_reduce(wsum[:], exo[:, :, 0:E], AX.X, ALU.add).then_inc(rt.sem, 1)
                return count

            def mask_low(n, front_next):
                wait(dve, lg_done, n, 1)
                dve.tensor_copy(low[:], lg[0:LROWS]).then_inc(low_split.sem, 1)
                wait(dve, low_split, n, 1)
                dve.tensor_tensor(low[64:96, :], lg[64:96], low[64:96, :].bitcast(F32),
                                  ALU.subtract).then_inc(low_split.sem, 1)
                if front_next:
                    wait(dve, norm_out, n + 1, 32)
                wait(dve, low_split, n, 2)
                for q, (dst, src) in enumerate(((low1, pa[1][:]), (low2, pa[0][:]))):
                    wait(dve, mask_ps, n, q + 1)
                    dve.tensor_tensor(dst, low[:].bitcast(F32), src[0:LROWS],
                                      ALU.mult).then_inc(low_masked.sem, 1)

            def experts(n):
                wait(dve, rho_done, n, 1)
                for f in range(FT):
                    wait(dve, z2_ps, n, f + 1)
                    dve.scalar_tensor_tensor(r2[:, f % 2, :], z_bank[f % 4][:], 0.0, rho, ALU.max,
                                             ALU.mult).then_inc(g_step.sem, 1)
                    wait(dve, g_step, n, 2 * f + 1)
                    dve.tensor_tensor(g[:, f % 4, :], g[:, f % 4, :], r2[:, f % 2, :], ALU.add).then_inc(g_step.sem, 1)

            def finish(n):
                wait(dve, out_done, n, out_done.per)
                wait(dve, wo_mm, n, FT)
                for t in range(NT):
                    dve.scalar_tensor_tensor(tg[:, t // 2, t % 2 * C:(t % 2 + 1) * C],
                                             pa[t // 2][:, t % 2 * C:(t % 2 + 1) * C], w1[:, t:t + 1], gb_now,
                                             ALU.mult, ALU.mult).then_inc(scaled.sem, 1)
                for b in range(2):
                    wait(dve, scaled, n + 1, 2 * b + 2)
                    dve.tensor_tensor(tg[:, b, :], tg[:, b, :],
                                      xr[:, 2 * b:2 * b + 2, :].rearrange("p t c -> p (t c)"),
                                      ALU.add).then_inc(fin.sem, 1)

            def ffn_rest(n, front_next):
                router(n)
                mask_low(n, front_next)
                wait(dve, rt, n, 23)
                dve.reciprocal(w1[:], wsum[:]).then_inc(rt.sem, 1)
                if front_next:
                    values(n + 1)
                experts(n)
                finish(n)

            setup_constants()
            ln1_stats(0, True)
            setup_silu()
            normalize_apply(0, tok, ln1_pool, hn_ready)
            setup_attention()
            setup_mods()
            split_h(0, hT_r, 2, hT_parts)
            for j in range(4):
                split_qk(0, j)
            split_norm(0)
            setup_gates()
            values(0)
            setup_late()

            def after_attend(n, front_next):
                if front_next:
                    split_qk(n + 1, 1)
                    split_qk(n + 1, 2)
                residual(n)
                if front_next:
                    split_qk(n + 1, 3)
                normalize_apply(n, xr, ln2_pool, h2n_ready[0])
                h2_copy(n)
                split_h(n, h2_r, 1, h2_parts)
                if front_next:
                    split_norm(n + 1)
                ffn_rest(n, front_next)

            with dve.Fori(0, NB - 1) as i:
                attend(i, True)
                after_attend(i, True)
            attend(NB - 1, False)
            after_attend(NB - 1, False)

        @block.gpsimd
        def _(pool):
            def setup():
                pool.memset(low_raw, 0.0).then_inc(set_pool.sem, 1)
                pool.memset(mk1[:], 0.0).then_inc(set_pool.sem, 1)
                pool.memset(mk2[:], 0.0).then_inc(set_pool.sem, 1)
                pool.wait_ge(ld_late.sem, 16 * LATE_LOADS)
                pool.wait_ge(set_pool.sem, 3)
                for half, mk in enumerate((mk1, mk2)):
                    for q in range(3):
                        pool.tensor_copy(mk[:, :, 32 * q:32 * q + LORA],
                                         lora_raw[:, 4 * half:4 * half + 4].rearrange("p t e r -> p t (e r)"))\
                            .then_inc(set_pool.sem, 1)

            def rstd_of(n, vec, sem):
                wait(pool, vec, n, 2 * NT)
                pool.tensor_tensor(neg_mean[:], mv[:, :, 0], neg_one[:], ALU.mult).then_inc(sem.sem, 1)
                pool.tensor_tensor(var_eps[:], mv[:, :, 1], eps[:], ALU.add).then_inc(sem.sem, 1)
                wait(pool, sem, n, 2)
                pool.tensor_tensor(rstd[:], var_eps[:], neg_half[:], ALU.pow).then_inc(sem.sem, 1)
                wait(pool, sem, n, 3)
                pool.tensor_tensor(shift[:], neg_mean[:], rstd[:], ALU.mult).then_inc(sem.sem, 1)

            def attend(n, front_next):
                row = n // BLOCKS_PER_ROW
                src = mod2[:, row, 0:2 * C] if isinstance(n, int) else \
                    mod2[:, bass.ds(row, 1), 0:2 * C].rearrange("p o c -> p (o c)")
                pool.tensor_copy(mod2_now[:], src).then_inc(mod2_set.sem, 1)
                if front_next:
                    rstd_of(n + 1, ln1_vec, ln1_pool)

            def residual(n):
                wait(pool, xr_loaded, n, 16)
                wait(pool, mod2_set, n, 1)
                two = xr[:]
                pool.tensor_tensor(two, two, over_tiles(bpg_now, NT), ALU.add).then_inc(xr_biased.sem, 1)

            pool.wait_ge(set_const.sem, 3)
            rstd_of(0, ln1_vec, ln1_pool)
            setup()
            pool.wait_ge(set_mod.sem, 4)
            pool.wait_ge(set_gate.sem, 11)
            with pool.Fori(0, NB - 1) as i:
                attend(i, True)
                residual(i)
                rstd_of(i, ln2_vec, ln2_pool)
                wait(pool, scaled, i + 1, NT)
            attend(NB - 1, False)
            residual(NB - 1)
            rstd_of(NB - 1, ln2_vec, ln2_pool)


AHEAD = {1: 2, 2: 2, 3: 1, 4: 1, 5: 1, 6: 1, 7: 1, 8: 1, 9: 1, 10: 1}
assert sum(AHEAD.values()) == 2 * TILES
ATTN_LOADS = 8
LATE_LOADS = 5 + E


def constants():
    import numpy as np
    r = np.arange(P)
    ident = np.eye(P, dtype=np.float32)
    causal = np.where(r[:, None] <= r[None, :], np.finfo(np.float32).max, 0).astype(np.float32)
    headsum = np.zeros((P, VA), np.float32)
    for p in range(P):
        h = p // DH
        headsum[p, h % 2 * GROUP + h // 2] = 1
    prio = np.broadcast_to(np.arange(E, 0, -1, dtype=np.float32), (P, E))
    consts = np.concatenate([ident, causal, headsum, prio], 1)
    rows = np.zeros((4, 2 * M), np.float32)
    for part in range(2):
        for a in range(2):
            rows[2 * part + a, a * M:(a + 1) * M] = -0.5
    return {"consts": np.ascontiguousarray(consts), "norm_rows": rows}


_INS = ['L0_attn_x', 'L0_attn_W_attn', 'L0_attn_b_attn', 'L0_attn_W_proj', 'L0_attn_b_proj', 'L0_attn_omega',
        'L0_ffn_Wg', 'L0_ffn_bg', 'L0_ffn_Wi', 'L0_ffn_Wo', 'L0_ffn_A', 'L0_ffn_B', 'L0_c', 'L0_wmod',
        'consts', 'norm_rows']


def kernel(**inputs):
    import numpy as np
    import concourse.bacc as bacc
    from concourse.bass_utils import run_bass_kernel_spmd

    nc = bacc.Bacc("TRN2", target_bir_lowering=False, num_devices=1)
    inputs = {**inputs, **constants()}
    arrays, args = {}, []
    for name in _INS:
        a = np.ascontiguousarray(inputs[name])
        arrays[f"in_{name}"] = a
        args.append(nc.dram_tensor(f"in_{name}", a.shape, mybir.dt.from_np(a.dtype), kind="ExternalInput").ap())
    out = nc.dram_tensor("out_x", (B, SEQ, C), F32, kind="ExternalOutput").ap()
    parts_out = nc.dram_tensor("qk_parts", (2, 4, P, T), F32, kind="Internal").ap()
    norms_out = nc.dram_tensor("norm_parts", (2, P, T), F32, kind="Internal").ap()
    build(nc, *args, out, parts_out, norms_out)
    r = run_bass_kernel_spmd(nc, [arrays], core_ids=[0])
    return r.results[0]["out_x"]
```

```python
from contextlib import ExitStack

import concourse.bass as bass
from concourse import mybir

P = 128
B, SEQ, C = 2, 2048, 256
H, DH, M = 16, 16, 128
F, E, R = 1024, 4, 4
T = 512
NT = T // P
KT = C // P
FT = F // P
NB = B * SEQ // T
BLOCKS_PER_ROW = SEQ // T
PAIRS = H // 2
GROUP = 4
GROUPS = H // GROUP
VA = P // GROUP
PAIR_ROWS = 2 * DH
XROWS = 3 * PAIR_ROWS + 4
LORA = E * R
LROWS = 96
LOGIT_ROW = 96
EPS_LN = 1e-5
EPS_DEN = 1e-6 * M
Q_SCALE = DH ** -0.5
TILES = 6
PAD = -3.0e38
AHEAD = {0: 1, 1: 1, 2: 2, 3: 1, 5: 1, 6: 1, 7: 1, 8: 1, 9: 2, 10: 1}
assert sum(AHEAD.values()) == 2 * TILES
QK_MOVES = (slice(0, 2), slice(2, 3), slice(3, 4))
ATTN_LOADS = 8
LATE_LOADS = 5 + E

ALU = mybir.AluOpType
ACT = mybir.ActivationFunctionType
AX = mybir.AxisListType
F32 = mybir.dt.float32
F32R = mybir.dt.float32r

CONSTS = {"ident": P, "causal": P, "headsum": VA, "prio": E}


class Signal:

    def __init__(self, sem, per):
        self.sem, self.per = sem, per

    def at(self, n, c):
        return n * self.per + c


def wait(eng, signal, n, c):
    eng.wait_ge(signal.sem, signal.at(n, c))


def build(nc, x, w_attn, b_attn, w_proj, b_proj, omega, wg, bg, wi, wo, lora_a, lora_b, cond, wmod,
          consts, norm_rows, out, parts_out, norms_out):
    ctx = ExitStack()
    with ctx:
        def sb(name, shape, dt=F32):
            return ctx.enter_context(nc.sbuf_tensor(name, shape, dt))

        def sig(name, per=0):
            return Signal(ctx.enter_context(nc.semaphore(name)), per)

        const = sb("const", [P, sum(CONSTS.values())])
        at, cols = 0, {}
        for name, width in CONSTS.items():
            cols[name] = const[:, at:at + width]
            at += width
        ident, causal, headsum, prio = (cols[name] for name in CONSTS)
        wa_r, wa_l = sb("wa_r", [P, KT, 3 * C], F32R), sb("wa_l", [P, KT, 3 * C], F32R)
        wi_r, wi_l = sb("wi_r", [P, KT, F], F32R), sb("wi_l", [P, KT, F], F32R)
        wo_r, wo_l = sb("wo_r", [P, FT, C], F32R), sb("wo_l", [P, FT, C], F32R)
        wp_ga = sb("wp_ga", [P, B, KT, C])
        low_t = sb("low_t", [P, KT, P])
        lora_w = sb("lora_w", [LROWS, F], F32R)
        omega_x = sb("omega_x", [XROWS, 2 * M], F32R)
        om_r, om_l = sb("om_r", [DH, M], F32R), sb("om_l", [DH, M], F32R)
        nrow_r = sb("nrow_r", [4, 2 * M], F32R)
        qk_bias = sb("qk_bias", [P, 4])
        v_bias = sb("v_bias", [P, C])
        bg_row = sb("bg_row", [P, E])
        neg_half = sb("neg_half", [P, NT])
        mod1 = sb("mod1", [P, B, 2 * KT])
        mod2 = sb("mod2", [P, B, 2 * C + 2 * KT])
        mod1_now = sb("mod1_now", [P, 2 * KT])
        mod2_now = sb("mod2_now", [P, 2 * C])
        mod2_cols = sb("mod2_cols", [P, 2 * KT])
        gb_now, bpg_now = (mod2_now[:, k * C:(k + 1) * C] for k in range(2))
        cT, sT = sb("cT", [P, KT, B]), sb("sT", [P, KT, B])

        tok = sb("tok", [P, NT, C])
        xr = sb("xr", [P, NT, C])
        stats, mv = sb("stats", [P, NT, 6]), sb("mv", [P, NT, 2])
        var_eps, rstd = sb("var_eps", [P, NT]), sb("rstd", [P, NT])
        neg_mean, shift = sb("neg_mean", [P, NT]), sb("shift", [P, NT])
        h_r, h_l = sb("h_r", [P, KT, T], F32R), sb("h_l", [P, KT, T], F32R)
        qk_r, qk_l = sb("qk_r", [P, 4, T], F32R), sb("qk_l", [P, 4, T], F32R)
        norm_r, norm_l = sb("norm_r", [P, T], F32R), sb("norm_l", [P, T], F32R)
        xq = sb("xq", [XROWS, 2, PAIRS, T], F32R)
        v_ones = sb("v_ones", [P, NT, H, VA])

        phq = sb("phq", [P, 2, GROUP, T])
        phkT = sb("phkT", [P, 2, 2, T])
        am_phk = sb("am_phk", [P, 3, GROUP, T])
        am = am_phk[:, 0]
        prod_sb = sb("prod_sb", [P, NT, 2, P])
        s_sb = sb("s_sb", [P, NT, P])
        oT_sb = s_sb
        state = sb("state", [P, 2, GROUPS, P])
        den, rden = sb("den", [P, NT, GROUP]), sb("rden", [P, NT, GROUP])

        tg = sb("tg", [P, 2, 2 * C])
        low1, low2 = norm_r[0:LROWS], norm_l[0:LROWS]
        mk1, mk2 = sb("mk1", [P, NT, LROWS]), sb("mk2", [P, NT, LROWS])
        route = sb("route", [P, 8, NT, E])
        rmax = sb("rmax", [P, 4, NT])
        ex, exo = sb("ex", [P, NT, E + 1]), sb("exo", [P, NT, E + 1])
        wsum, w1 = sb("wsum", [P, NT]), sb("w1", [P, NT])

        qk_sq = phq[:, 0]
        g, rho = phq[:, 1], am[:, 3]
        yT = phkT[:, 0]
        y = tg[:].rearrange("p b (t c) -> p (b t) c", t=2)
        g_r, g_l, low = qk_r[:, 0:3], qk_l[:, 0:3], qk_r[0:LROWS, 3]
        r2, lg = am[:, 0:2], am[:, 2]
        h_f = am_phk[:, 1, 0:2]

        flat = lambda ap: ap.rearrange("p a t -> p (a t)")
        wmod_raw = [[flat(phq[:, 0])[:, 2 * k * C:2 * (k + 1) * C] for k in range(KT)],
                    [flat(phq[:, 1])[:, 4 * k * C:4 * (k + 1) * C] for k in range(KT)]]
        wa_raw = [flat(phkT[:, k])[:, 0:3 * C] for k in range(KT)]
        wi_raw = [flat(am_phk[:, 2, 2 * k:2 * k + 2]) for k in range(2)]
        wo_raw = [flat(am[:, 2 * k:2 * k + 2]) for k in range(KT)]
        low_raw = tg[:, 1, 0:C]
        om_f, nrow_f = am_phk[0:DH, 1, 3, 0:M], am_phk[0:4, 1, 3, M:3 * M]
        bp_row = flat(phkT[:, 0])[:, 3 * C:4 * C]
        gate_tmp = [am_phk[:, 1, 2 + q].rearrange("p (b c) -> p b c", b=B) for q in range(2)]
        wp = flat(s_sb[:]).rearrange("p (k c) -> p k c", k=KT)
        ga_rows = prod_sb[:, 1:3].rearrange("p b k m -> p b (k m)")
        lora_raw = prod_sb[:, 0, 0, :].rearrange("p (t e r) -> p t e r", t=FT, e=E)
        s_rep = tg[:].rearrange("p b n -> p (b n)")[:, 0:KT * B * P].rearrange("p (k b m) -> p k b m", k=KT, b=B)

        def bank(name):
            return ctx.enter_context(nc.psum_tensor(name, [P, 512], F32))

        ring = [bank(f"ring{i}") for i in range(4)]
        pa = [bank("pa0"), bank("pa1")]
        prod = ctx.enter_context(nc.psum_tensor("prod", [P, NT, 2, P], F32))
        pb = [prod[:, 2 * b:2 * b + 2].rearrange("p c k m -> p (c k m)") for b in range(2)]
        qk_bank = [pa[0], pa[1], ring[2], ring[3]]
        z_bank = [ring[3], ring[1], ring[0], ring[2]]
        score_bank = lambda q, a: (pa if q else pb)[a]
        proj_bank = lambda tile: pb[tile % 2] if tile < 2 * TILES else ring[tile % 4]

        ld_cond, ld_x, ld_const = sig("ld_cond"), sig("ld_x"), sig("ld_const")
        ld_mod = [sig("ld_mod0"), sig("ld_mod1")]
        ld_attn, ld_late, ld_low = sig("ld_attn"), sig("ld_late"), sig("ld_low")
        om_parts, om_moved = sig("om_parts"), sig("om_moved")
        set_const, set_silu, set_wa, set_mod = (sig("set_" + x) for x in ("const", "silu", "wa", "mod"))
        set_gate = [sig("set_ga"), sig("set_gb")]
        set_act, mods_ps, gates_ps, set_pool = sig("set_act"), sig("mods_ps"), sig("gates_ps"), sig("set_pool")
        wp_done = sig("wp_done")
        bias_gated = sig("bias_gated")
        late_pe, late_vec, late_act = sig("late_pe"), sig("late_vec"), sig("late_act")
        x_loaded, tok_free = sig("x_loaded", 16), sig("tok_free", 1)
        ln1_vec, ln1_pool, hn_ready = sig("ln1_vec", 10), sig("ln1_pool", 2), sig("hn_ready", 4)
        hT_ps, hT_r, hT_parts = sig("hT_ps", 2), sig("hT_r", 4), sig("hT_parts", 2)
        qk_ps, sq_ready = sig("qk_ps", 4), sig("sq_ready", 4)
        qk_split = sig("qk_split", 4)
        norm_mm, norm_full, norm_split = sig("norm_mm", 1), sig("norm_full", 1), sig("norm_split", 1)
        qk_out = [sig(name, 2 * 16) for name in ("q_out", "k0_out", "k1_out")]
        norm_out = sig("norm_out", 2 * 16)
        moved, moved_late = sig("moved", 10 * 16), sig("moved_late", 3 * 16)
        v_ps, v_done = sig("v_ps", 2), sig("v_done", 2)
        proj_ps, exp_done = sig("proj_ps", PAIRS * TILES), sig("exp_done", PAIRS * TILES)
        a_ps, am_done = sig("a_ps", H), sig("am_done", H)
        prod_ps, d_ps = sig("prod_ps", GROUPS), sig("d_ps", GROUPS)
        copied = [sig("copied0", GROUPS), sig("copied1", GROUPS)]
        s_step, read_ps = sig("s_step", (NT + 1) * GROUPS), sig("read_ps", GROUPS)
        oT_added, o_ps, y_step = sig("oT_added", GROUPS), sig("o_ps", GROUPS), sig("y_step", 3 * GROUPS)
        mod2_set, mod1_set, mod2c_set = sig("mod2_set", 1), sig("mod1_set", 1), sig("mod2c_set", 1)
        yT_ps, yT_done, prj_ps = sig("yT_ps", 2), sig("yT_done", 2), sig("prj_ps", 2)
        xr_loaded, xr_biased, x2_step = sig("xr_loaded", 16), sig("xr_biased", 1), sig("x2_step", 2)
        ln2_vec, ln2_pool = sig("ln2_vec", 10), sig("ln2_pool", 2)
        h2n_ready = [sig("h2n_vec", 2), sig("h2n_act", 2)]
        h2_ps = sig("h2_ps", 2)
        h2_full, h2_r, h2_parts = [sig("h2_full0", 1), sig("h2_full1", 1)], sig("h2_r", 2), sig("h2_parts", 2)
        lg_ps, lg_done, lt_ps = sig("lg_ps", 1), sig("lg_done", 1), sig("lt_ps", 1)
        low_high, low_split, low_masked = sig("low_high", 1), sig("low_split", 1), sig("low_masked", 2)
        rt, rt_exp, mask_ps = sig("rt", 24), sig("rt_exp", 1), sig("mask_ps", 2)
        rho_ps, rho_done = sig("rho_ps", 1), sig("rho_done", 1)
        z1_ps, r1_done, z2_ps = sig("z1_ps", FT), sig("r1_done", FT), sig("z2_ps", FT)
        r2_done, g_sum, g_high, g_low = (sig(name, FT) for name in ("r2_done", "g_sum", "g_high", "g_low"))
        wo_mm, fin = sig("wo_mm", FT), sig("fin", 2)
        scaled = sig("scaled", NT)
        out_done = sig("out_done", 32)

        x_rows = x.rearrange("b (n t p) c -> (b n) p t c", p=P, t=NT)
        out_rows = out.rearrange("b (n t p) c -> (b n) p t c", p=P, t=NT)

        def block_rows(rows, n):
            return rows[n] if isinstance(n, int) else rows[bass.ds(n, 1)].rearrange("o p t c -> p (o t) c")

        def over_tiles(row, k):
            return row.rearrange("p (o w) -> p o w", o=1).broadcast_to([P, k, row.shape[1]])

        def last_bc(ap, k):
            return ap.broadcast_to([ap.shape[0], ap.shape[1], k])

        block = ctx.enter_context(nc.Block())

        @block.sync
        def _(sp):
            def move(dst, src):
                return sp.dma_start(dst.bitcast(F32), src.bitcast(F32))

            def load(signal, *pairs):
                for dst, src in pairs:
                    sp.dma_start(dst, src, allow_slow_non_contiguous=True).then_inc(signal.sem, 16)

            row_bc = lambda ap, w: ap.rearrange("(o c) -> o c", o=1).broadcast_to([P, w])
            load(ld_cond, *((cT[:, k, :], cond[:, k * P:(k + 1) * P].rearrange("b p -> p b")) for k in range(KT)))
            load(ld_x, (tok[:], x_rows[0]))
            load(ld_const, (const[:], consts))
            for half, w in enumerate((slice(0, 2 * C), slice(2 * C, 6 * C))):
                load(ld_mod[half], *((wmod_raw[half][k], wmod[k * P:(k + 1) * P, w]) for k in range(KT)))
            load(ld_attn, (om_f, omega), (nrow_f, norm_rows),
                 (wa_raw[0], w_attn[0:P, :]), (wa_raw[1], w_attn[P:C, :]),
                 (qk_bias[:], b_attn[0:2 * C].rearrange("(j p) -> p j", p=P)),
                 (v_bias[:], row_bc(b_attn[2 * C:3 * C], C)), (bp_row, row_bc(b_proj, C)),
                 (bg_row[:], row_bc(bg, E)))
            late = [(wi_raw[k].rearrange("p (t d) -> p t d", t=FT // 2),
                     wi.rearrange("(k t p) d -> k p t d", k=2, p=P)[k]) for k in range(2)]
            late += [(wo_raw[k], wo[k * P:(k + 1) * P, :]) for k in range(KT)]
            late += [(wp, w_proj.rearrange("(k p) n -> p k n", p=P))]
            late += [(lora_raw[:, :, e, :], lora_b[e].rearrange("(t p) r -> p t r", p=P)) for e in range(E)]
            assert len(late) == LATE_LOADS
            for dst, src in late:
                sp.dma_start(dst, src).then_inc(ld_late.sem, 16)
            sp.dma_start(xr[:], x_rows[0]).then_inc(xr_loaded.sem, 16)
            sp.wait_ge(set_pool.sem, 1)
            a_rows = lora_a.rearrange("e r d -> (e r) d")
            for q in range(3):
                sp.dma_start(low_raw[32 * q:32 * q + LORA, :], a_rows).then_inc(ld_low.sem, 16)
            sp.dma_start(low_raw[LOGIT_ROW:LOGIT_ROW + E, :], wg).then_inc(ld_low.sem, 16)
            sp.wait_ge(om_parts.sem, 4)
            for a in range(2):
                for k, part in enumerate((om_r, om_l, om_r)):
                    row = k * PAIR_ROWS + a * DH
                    move(omega_x[row:row + DH, a * M:(a + 1) * M], part[:]).then_inc(om_moved.sem, 16)
            move(omega_x[3 * PAIR_ROWS:XROWS, :], nrow_r[:]).then_inc(om_moved.sem, 16)
            sp.sem_inc(out_done.sem, out_done.per)
            sp.sem_inc(scaled.sem, scaled.per)

            def front_moves(n):
                def send(k):
                    tiles = QK_MOVES[k]
                    wait(sp, qk_split, n, tiles.stop)
                    for part, src in enumerate((qk_r, qk_l)):
                        sp.dma_start(parts_out[part, tiles].rearrange("j p t -> p j t"),
                                     src[:, tiles, :].bitcast(F32)).then_inc(qk_out[k].sem, 16)

                def fetch(k, signal):
                    wait(sp, qk_out[k], n, 32)
                    tiles = QK_MOVES[k]
                    kind, first = tiles.start // 2, tiles.start % 2 * (PAIRS // 2)
                    pairs = slice(first, first + (tiles.stop - tiles.start) * (PAIRS // 2))
                    for copy, part in enumerate((0, 0, 1)):
                        src = parts_out[part, tiles].rearrange("j (i r) t -> r (j i) t", r=PAIR_ROWS)
                        sp.dma_start(xq[copy * PAIR_ROWS:(copy + 1) * PAIR_ROWS, kind, pairs].bitcast(F32),
                                     src).then_inc(signal.sem, 16)

                send(0)
                send(1)
                fetch(0, moved)
                send(2)
                fetch(1, moved)
                wait(sp, norm_split, n, 1)
                for part, src in enumerate((norm_r, norm_l)):
                    sp.dma_start(norms_out[part], src[:].bitcast(F32)).then_inc(norm_out.sem, 16)
                wait(sp, norm_out, n, 32)
                for part in range(2):
                    row = 3 * PAIR_ROWS + 2 * part
                    for a in range(2):
                        src = norms_out[part].rearrange("(j r) t -> r j t", r=VA)[a * GROUP:(a + 1) * GROUP]
                        sp.dma_start(xq[row + a:row + a + 1].rearrange("o k (f i) t -> o (k f) i t", f=2).bitcast(F32),
                                     src.rearrange("i j t -> j i t").rearrange("(o j) i t -> o j i t", o=1))\
                            .then_inc(moved.sem, 16)
                fetch(2, moved_late)

            def ffn_stores(n):
                dst = block_rows(out_rows, n)
                for b in range(2):
                    wait(sp, fin, n, b + 1)
                    sp.dma_start(dst[:, 2 * b:2 * b + 2, :],
                                 tg[:, b, :].rearrange("p (t c) -> p t c", t=2)).then_inc(out_done.sem, 16)

            front_moves(0)
            with sp.Fori(0, NB - 1) as i:
                wait(sp, tok_free, i, 1)
                sp.dma_start(tok[:], block_rows(x_rows, i + 1)).then_inc(x_loaded.sem, 16)
                front_moves(i + 1)
                ffn_stores(i)
                sp.dma_start(xr[:], block_rows(x_rows, i + 1)).then_inc(xr_loaded.sem, 16)
            ffn_stores(NB - 1)
            wait(sp, out_done, NB, out_done.per)

        @block.tensor
        def _(pe):
            def split3(dst, w_r, w_l, v_r, v_l, first, last, shared=False):
                pe.matmul(dst, w_r, v_r, start=first, stop=False, skip_group_check=shared)
                pe.matmul(dst, w_l, v_r, start=False, stop=False, skip_group_check=shared)
                return pe.matmul(dst, w_r, v_l, start=False, stop=last, skip_group_check=shared)

            def setup_mods(step):
                pe.wait_ge(ld_mod[step].sem, 16 * KT)
                pe.wait_ge(set_silu.sem, 4)
                for m, which in enumerate((1, 0, 4, 3)):
                    if m // 2 != step:
                        continue
                    for half in range(KT):
                        col = (m * KT + half) * B
                        for k in range(KT):
                            mm = pe.matmul(pa[0][:, col:col + B],
                                      wmod_raw[step][k][:, (which - 2 * step) * C + half * P:][:, 0:P],
                                      sT[:, k, :], start=k == 0, stop=k == KT - 1)
                mm.then_inc(mods_ps.sem, 1)

            def setup_gates():
                for which, dst in ((2, pb[0]), (5, pb[1])):
                    for b in range(B):
                        for k in range(KT):
                            mm = pe.matmul(dst[:, b * C:(b + 1) * C], s_rep[:, k, b, :],
                                           wmod_raw[1][k][:, (which - 2) * C:(which - 1) * C],
                                           start=k == 0, stop=k == KT - 1)
                    mm.then_inc(gates_ps.sem, 1)

            def transpose1(n):
                wait(pe, hn_ready, n, NT)
                for k in range(KT):
                    for t in range(NT):
                        mm = pe.transpose(ring[k][:, t * P:(t + 1) * P], tok[:, t, k * P:(k + 1) * P], ident)
                    mm.then_inc(hT_ps.sem, 1)

            def qk(n, j, ks=range(KT)):
                for k in ks:
                    if j == 0:
                        wait(pe, hT_parts, n, k + 1)
                    w = slice(j * P, (j + 1) * P)
                    mm = split3(qk_bank[j][:], wa_r[:, k, w], wa_l[:, k, w], h_r[:, k, :], h_l[:, k, :],
                                k == 0, k == KT - 1)
                if KT - 1 in ks:
                    mm.then_inc(qk_ps.sem, 1)

            def norms(n):
                wait(pe, sq_ready, n, 4)
                for j in range(4):
                    mm = pe.matmul(ring[0][j * VA:(j + 1) * VA, :], headsum, qk_sq[:, j, :], start=True, stop=True)
                mm.then_inc(norm_mm.sem, 1)

            def values(n):
                for t in range(NT):
                    dst = pb[t // 2][:, t % 2 * C:(t % 2 + 1) * C]
                    tt = slice(t * P, (t + 1) * P)
                    for k in range(KT):
                        mm = split3(dst, h_r[:, k, tt], h_l[:, k, tt],
                                    wa_r[:, k, 2 * C:3 * C], wa_l[:, k, 2 * C:3 * C], k == 0, k == KT - 1)
                    if t % 2:
                        mm.then_inc(v_ps.sem, 1)

            def setup_late():
                pe.wait_ge(ld_late.sem, 16 * LATE_LOADS)
                wait(pe, norm_split, 0, 1)
                for k in range(KT):
                    for half in range(2):
                        for t in range(4):
                            mm = pe.transpose(ring[2 * k + half][:, t * P:(t + 1) * P],
                                              wi_raw[half][:, t * C + k * P:t * C + (k + 1) * P], ident)
                        mm.then_inc(late_pe.sem, 1)
                pe.wait_ge(set_mod.sem, 4)
                for gate in set_gate:
                    pe.wait_ge(gate.sem, 3)
                for q in range(4):
                    for t in range(2):
                        for k in range(KT):
                            f = (2 * q + t) * P
                            mm = pe.transpose((*pa, *pb)[q][:, (t * KT + k) * P:(t * KT + k + 1) * P],
                                              wo_raw[k][:, f:f + P], ident)
                    mm.then_inc(late_pe.sem, 1)
                pe.wait_ge(ld_low.sem, 16 * 4)
                pe.wait_ge(late_vec.sem, 1)
                for k in range(KT):
                    mm = pe.transpose(ring[0][:, k * P:(k + 1) * P], low_raw[:, k * P:(k + 1) * P], ident)
                mm.then_inc(late_pe.sem, 1)
                pe.wait_ge(set_pool.sem, 9)
                pe.wait_ge(late_vec.sem, 3)
                for half, src in enumerate((mk1, mk2)):
                    for t in range(4):
                        mm = pe.transpose(ring[1 + half][0:LROWS, t * P:(t + 1) * P], src[:, t, :], ident)
                    mm.then_inc(late_pe.sem, 1)
                pe.wait_ge(late_act.sem, 8)
                pe.wait_ge(late_vec.sem, 8)

            def features(n, p, tiles=range(TILES)):
                for k in tiles:
                    tile = p * TILES + k
                    dst = proj_bank(tile)
                    if tile == 0:
                        wait(pe, moved, n, moved.per)
                    if tile == PAIRS // 2 * TILES:
                        wait(pe, moved_late, n, moved_late.per)
                    if 2 <= tile < 2 * TILES:
                        wait(pe, exp_done, n, tile - 1)
                    if tile >= 2 * TILES + 4:
                        wait(pe, exp_done, n, tile - 3)
                    if k < 4:
                        mm = pe.matmul(dst[:], omega_x[:, k // 2 * M:(k // 2 + 1) * M], xq[:, k % 2, p, :],
                                       start=True, stop=True)
                    else:
                        for c in range(2):
                            t = (2 * (k - 4) + c) * P
                            mm = pe.matmul(dst[:, c * 2 * M:(c + 1) * 2 * M], xq[:, 1, p, t:t + P], omega_x[:],
                                           start=True, stop=True)
                    mm.then_inc(proj_ps.sem, 1)

            def scores(n, q, a):
                if q:
                    wait(pe, exp_done, n, q * TILES + 2 * a + 2)
                if q == 0:
                    wait(pe, exp_done, n, 2 * TILES)
                if q == 1:
                    wait(pe, scaled, n, 2 * a + 2)
                if q > 1:
                    wait(pe, am_done, n, 2 * (q - 1) + a + 1)
                for c in range(NT):
                    tt = slice(c * P, (c + 1) * P)
                    mm = pe.matmul(score_bank(q, a)[:, tt], phkT[:, q % 2, a, tt],
                                   phq[:, q // 2 % 2, 2 * (q % 2) + a, tt], start=True, stop=True)
                mm.then_inc(a_ps.sem, 1)

            def products(n, gr):
                if gr == 0:
                    wait(pe, v_done, n, 2)
                else:
                    wait(pe, y_step, n, 3 * gr)
                wait(pe, am_done, n, GROUP * (gr + 1))
                wait(pe, exp_done, n, 2 * TILES * (gr + 1))
                for j in range(GROUP):
                    rows = slice(j * VA, (j + 1) * VA)
                    for c in range(NT):
                        both = am_phk[:, 0:2 + gr % 2:1 + gr % 2, j, c * P:(c + 1) * P]
                        mm = pe.matmul(prod[rows, c], v_ones[:, c, GROUP * gr + j, :], both, start=True, stop=True)
                mm.then_inc(prod_ps.sem, 1)

            def state_transpose(n, gr):
                for c in range(NT):
                    if c % 2 == 0:
                        wait(pe, copied[c // 2], n, gr + 1)
                    mm = pe.transpose(prod[:, c, 1, :], prod_sb[:, c, 1, :], ident)
                mm.then_inc(d_ps.sem, 1)

            def state_reads(n, gr):
                wait(pe, s_step, n, (NT + 1) * (gr + 1))
                for j in range(GROUP):
                    rows = slice(j * VA, (j + 1) * VA)
                    for c in range(NT):
                        mm = pe.matmul(prod[rows, c, 1, :], s_sb[:, c, rows], phq[:, gr % 2, j, c * P:(c + 1) * P],
                                       start=True, stop=True)
                mm.then_inc(read_ps.sem, 1)

            def out_transpose(n, gr):
                wait(pe, oT_added, n, gr + 1)
                for c in range(NT):
                    mm = pe.transpose(prod[:, c, 0, :], oT_sb[:, c, :], ident)
                mm.then_inc(o_ps.sem, 1)

            def attend(n, front_next):
                scores(n, 0, 0)
                scores(n, 0, 1)
                features(n, 2, range(4))
                scores(n, 1, 0)
                features(n, 2, range(4, TILES))
                scores(n, 1, 1)
                features(n, 3, range(4))
                for gr in range(GROUPS):
                    more = gr + 1 < GROUPS
                    q = 2 * gr + 2
                    products(n, gr)
                    if q + 1 < PAIRS:
                        features(n, q + 1, range(4, TILES))
                    if more:
                        scores(n, q, 0)
                    elif front_next:
                        qk(n + 1, 0, [0])
                        qk(n + 1, 1, [0])
                    state_transpose(n, gr)
                    if more:
                        scores(n, q, 1)
                        scores(n, q + 1, 0)
                    elif front_next:
                        qk(n + 1, 0, [1])
                        qk(n + 1, 1, [1])
                        qk(n + 1, 2, [0])
                    state_reads(n, gr)
                    if q + 2 < PAIRS:
                        features(n, q + 2, range(4))
                    elif more:
                        scores(n, q + 1, 1)
                    elif front_next:
                        qk(n + 1, 2, [1])
                    out_transpose(n, gr)
                    if q + 2 < PAIRS:
                        features(n, q + 2, range(4, TILES))
                        scores(n, q + 1, 1)
                        features(n, q + 3, range(4))
                    elif more and front_next:
                        wait(pe, exp_done, n, PAIRS * TILES)
                        transpose1(n + 1)

            def y_transpose(n):
                wait(pe, y_step, n, 3 * GROUPS)
                for k in range(KT):
                    for t in range(NT):
                        mm = pe.transpose(ring[k][:, t * P:(t + 1) * P], y[:, t, k * P:(k + 1) * P], ident)
                    mm.then_inc(yT_ps.sem, 1)

            def projection(n, front_next):
                wait(pe, yT_done, n, KT)
                if front_next:
                    wait(pe, qk_split, n + 1, 2)
                row = n // BLOCKS_PER_ROW
                for t in range(NT):
                    dst = pa[t // 2][:, t % 2 * C:(t % 2 + 1) * C]
                    for k in range(KT):
                        w = wp_ga[:, row, k, :] if isinstance(n, int) else \
                            wp_ga[:, bass.ds(row, 1), k, :].rearrange("p o c -> p (o c)")
                        mm = pe.matmul(dst, yT[:, k, t * P:(t + 1) * P], w, start=k == 0, stop=k == KT - 1)
                    if t % 2:
                        mm.then_inc(prj_ps.sem, 1)

            def base(n, f, ks=range(KT)):
                if f >= 4:
                    wait(pe, r2_done, n, f - 3)
                w = slice(f * P, (f + 1) * P)
                for k in ks:
                    if f == 0:
                        wait(pe, h2_parts, n, k + 1)
                    split3(z_bank[f % 4][:], wi_r[:, k, w], wi_l[:, k, w], h_r[:, k, :], h_l[:, k, :], k == 0, False)

            def ffn_head(n, front_next):
                for t in range(NT):
                    wait(pe, h2n_ready[t // 2], n, t % 2 + 1)
                    for k, dst in enumerate((ring[3], ring[1])):
                        mm = pe.transpose(dst[:, t * P:(t + 1) * P], tok[:, t, k * P:(k + 1) * P], ident)
                        if t == NT - 1:
                            mm.then_inc(h2_ps.sem, 1)
                for k in range(KT):
                    wait(pe, h2_full[k], n, 1)
                    mm = pe.matmul(ring[2][:], low_t[:, k, :], h_f[:, k, :], start=k == 0, stop=k == KT - 1)
                    if k == 0:
                        mm.then_inc(tok_free.sem, 1)
                mm.then_inc(lg_ps.sem, 1)
                base(n, 0, [0])
                wait(pe, lg_done, n, 1)
                base(n, 0, [1])
                rows = slice(LOGIT_ROW, LOGIT_ROW + E)
                for t in range(NT):
                    mm = pe.transpose(pa[0][:, t * E:(t + 1) * E], lg[rows, t * P:(t + 1) * P], ident[rows, rows])
                mm.then_inc(lt_ps.sem, 1)
                base(n, 1)
                if front_next:
                    wait(pe, norm_split, n + 1, 1)
                base(n, 2)
                wait(pe, low_high, n, 1)
                base(n, 3)

            def masks(n):
                for src, need, dst in ((mk1, 18, pa[1]), (mk2, 21, pa[0])):
                    wait(pe, rt, n, need)
                    for t in range(NT):
                        mm = pe.transpose(dst[0:LROWS, t * P:(t + 1) * P], src[:, t, :], ident)
                    mm.then_inc(mask_ps.sem, 1)

            def ratio(n):
                for t in range(NT):
                    mm = pe.transpose(pa[1][:, t * P:(t + 1) * P], r2[:, 0, t * P:(t + 1) * P], ident)
                mm.then_inc(rho_ps.sem, 1)

            def experts(n, front_next):
                tile = 0
                if front_next:
                    wait(pe, v_done, n + 1, 2)
                for f in range(FT + 3):
                    if f < FT:
                        if f == 0:
                            wait(pe, low_masked, n, 1)
                        w = slice(f * P, (f + 1) * P)
                        pe.matmul(z_bank[f % 4][:], lora_w[:, w], low1, start=False,
                                  stop=True).then_inc(z1_ps.sem, 1)
                    if f == 0:
                        wait(pe, rt, n, 22)
                        ratio(n)
                    if 4 <= f + 2 < FT:
                        base(n, f + 2)
                    if 1 <= f <= FT:
                        if f == 1:
                            wait(pe, low_masked, n, 2)
                        wait(pe, r1_done, n, f)
                        w = slice((f - 1) * P, f * P)
                        pe.matmul(z_bank[(f - 1) % 4][:], lora_w[:, w], low2, start=False, stop=True,
                                  skip_group_check=True).then_inc(z2_ps.sem, 1)
                    if front_next:
                        for _ in range(AHEAD.get(f, 0)):
                            features(n + 1, tile // TILES, [tile % TILES])
                            tile += 1
                    if f >= 3:
                        k = f - 3
                        if k == 0:
                            wait(pe, rho_done, n, 1)
                        wait(pe, g_low, n, k + 1)
                        for t in range(NT):
                            tt = slice(t * P, (t + 1) * P)
                            mm = split3(pa[t // 2][:, t % 2 * C:(t % 2 + 1) * C], g_r[:, k % 3, tt], g_l[:, k % 3, tt],
                                        wo_r[:, k, :], wo_l[:, k, :], k == 0 and t % 2 == 0, k == FT - 1, True)
                        mm.then_inc(wo_mm.sem, 1)

            pe.wait_ge(ld_const.sem, 16)
            transpose1(0)
            setup_mods(0)
            pe.wait_ge(set_wa.sem, 4 * KT)
            pe.wait_ge(set_mod.sem, 2)
            for k in range(KT):
                for j in range(2):
                    qk(0, j, [k])
            for j in range(2, 4):
                qk(0, j)
            norms(0)
            values(0)
            wait(pe, qk_split, 0, 4)
            setup_mods(1)
            wait(pe, v_done, 0, 2)
            setup_gates()
            setup_late()
            pe.wait_ge(om_moved.sem, 16 * 7)
            pe.nop().then_inc(tok_free.sem, 1)
            pe.wait_ge(bias_gated.sem, 1)
            features(0, 0)
            features(0, 1)
            pe.wait_ge(late_act.sem, 11)
            pe.wait_ge(late_vec.sem, 10)
            pe.wait_ge(wp_done.sem, B)

            def after_attend(n, front_next):
                if front_next:
                    qk(n + 1, 3, [0])
                y_transpose(n)
                if front_next:
                    qk(n + 1, 3, [1])
                projection(n, front_next)
                if front_next:
                    norms(n + 1)
                    values(n + 1)
                ffn_head(n, front_next)
                masks(n)
                experts(n, front_next)

            with pe.Fori(0, NB - 1) as i:
                attend(i, True)
                after_attend(i, True)
            attend(NB - 1, False)
            after_attend(NB - 1, False)

        @block.scalar
        def _(act):
            def setup():
                act.wait_ge(ld_cond.sem, 16 * KT)
                act.activation(sT[:], cT[:], ACT.Exp, scale=-1.0).then_inc(set_act.sem, 1)
                act.wait_ge(ld_attn.sem, 16 * ATTN_LOADS)
                act.activation(qk_bias[:], qk_bias[:], ACT.Copy, scale=Q_SCALE).then_inc(set_act.sem, 1)

            def front_hT(n):
                wait(act, mod1_set, n, 1)
                for k in range(KT):
                    wait(act, hT_ps, n, k + 1)
                    for dst in (h_f, h_r):
                        act.activation(dst[:, k, :], ring[k][:], ACT.Identity, bias=mod1_now[:, KT + k:KT + k + 1],
                                       scale=mod1_now[:, k:k + 1]).then_inc(hT_r.sem, 1)

            def front_qk(n, j):
                wait(act, qk_ps, n, j + 1)
                act.activation(qk_r[:, j, :], qk_bank[j][:], ACT.Identity,
                               bias=qk_bias[:, j:j + 1])
                act.activation(qk_sq[:, j, :], qk_bank[j][:], ACT.Square,
                               bias=qk_bias[:, j:j + 1]).then_inc(sq_ready.sem, 1)

            def front_norm(n):
                wait(act, norm_mm, n, 1)
                act.activation(norm_r[:], ring[0][:], ACT.Copy).then_inc(norm_full.sem, 1)

            def setup_late():
                for q in range(4):
                    act.wait_ge(late_pe.sem, q + 1)
                    w = slice(q % 2 * T, (q % 2 + 1) * T)
                    act.activation(wi_r[:, q // 2, w], ring[q][:], ACT.Copy).then_inc(late_act.sem, 1)
                for q in range(4):
                    act.wait_ge(late_pe.sem, 5 + q)
                    act.activation(wo_r[:, 2 * q:2 * q + 2, :].rearrange("p t c -> p (t c)"), (*pa, *pb)[q][:],
                                   ACT.Copy).then_inc(late_act.sem, 1)
                act.wait_ge(late_pe.sem, 9)
                act.activation(low_t[:].rearrange("p k m -> p (k m)"), ring[0][:, 0:KT * P],
                               ACT.Copy).then_inc(late_act.sem, 1)
                for half in range(2):
                    act.wait_ge(late_pe.sem, 10 + half)
                    act.activation(lora_w[:, half * T:(half + 1) * T], ring[1 + half][0:LROWS, :],
                                   ACT.Copy).then_inc(late_act.sem, 1)

            def features(n, q, tiles):
                for k in tiles:
                    tile = q * TILES + k
                    wait(act, proj_ps, n, tile + 1)
                    slot = q // 2 % 2
                    if k >= 4:
                        c = 2 * (k - 4) * P
                        dst = am_phk[:, 1 + slot, 2 * (q % 2):2 * (q % 2) + 2, c:c + 2 * P]\
                            .rearrange("p a (c m) -> p c a m", c=2)
                        src = proj_bank(tile)[:].rearrange("p (c a m) -> p c a m", c=2, a=2)
                    else:
                        dst = (phq[:, slot, 2 * (q % 2) + k // 2, :], phkT[:, q % 2, k // 2, :])[k % 2]
                        src = proj_bank(tile)[:]
                    act.activation(dst, src, ACT.Exp).then_inc(exp_done.sem, 1)

            def attend(n, front_next):
                features(n, 2, range(TILES))
                for gr in range(GROUPS):
                    ahead = 2 * gr + 3
                    if ahead < PAIRS:
                        features(n, ahead, range(4))
                    wait(act, prod_ps, n, gr + 1)
                    act.activation(prod_sb[:, 0:2].rearrange("p c k m -> p (c k m)"), pb[0],
                                   ACT.Copy).then_inc(copied[0].sem, 1)
                    if ahead < PAIRS:
                        features(n, ahead, range(4, TILES))
                    if ahead + 1 < PAIRS:
                        features(n, ahead + 1, range(TILES))
                    if front_next and gr == GROUPS - 2:
                        front_hT(n + 1)

            def y_copy(n):
                for k in range(KT):
                    wait(act, yT_ps, n, k + 1)
                    act.activation(yT[:, k, :], ring[k][:], ACT.Copy).then_inc(yT_done.sem, 1)

            def ffn(n, front_next):
                wait(act, ln2_pool, n, 2)
                for t in range(2, NT):
                    act.activation(tok[:, t, :], xr[:, t, :], ACT.Identity, bias=shift[:, t:t + 1],
                                   scale=rstd[:, t:t + 1]).then_inc(h2n_ready[1].sem, 1)
                wait(act, mod2c_set, n, 1)
                wait(act, h2_ps, n, 1)
                act.activation(h_f[:, 0, :], ring[3][:], ACT.Identity, bias=mod2_cols[:, KT:KT + 1],
                               scale=mod2_cols[:, 0:1]).then_inc(h2_full[0].sem, 1)
                for k in range(KT):
                    wait(act, h2_full[k], n, 1)
                    act.activation(h_r[:, k, :], h_f[:, k, :], ACT.Copy).then_inc(h2_r.sem, 1)
                wait(act, lg_ps, n, 1)
                act.activation(lg, ring[2][:], ACT.Copy).then_inc(lg_done.sem, 1)
                if front_next:
                    for signal in qk_out:
                        wait(act, signal, n + 1, 32)
                act.activation(low, ring[2][0:LROWS, :], ACT.Copy).then_inc(low_high.sem, 1)
                wait(act, rt, n, 10)
                act.activation(exo[:], ex[:], ACT.Exp).then_inc(rt_exp.sem, 1)
                tile = 0
                for f in range(FT + 3):
                    if f < FT:
                        wait(act, z1_ps, n, f + 1)
                        if f >= 4:
                            wait(act, g_low, n, f - 3)
                        act.activation(g[:, f % 4, :], z_bank[f % 4][:], ACT.Relu).then_inc(r1_done.sem, 1)
                    if f == 0:
                        wait(act, rho_ps, n, 1)
                        act.activation(rho, pa[1][:], ACT.Copy).then_inc(rho_done.sem, 1)
                    for _ in range(AHEAD.get(f, 0) if front_next else 0):
                        features(n + 1, tile // TILES, [tile % TILES])
                        tile += 1
                    if 1 <= f <= FT:
                        k = f - 1
                        wait(act, g_sum, n, k + 1)
                        if k >= 3:
                            wait(act, wo_mm, n, k - 2)
                        act.activation(g_r[:, k % 3, :], g[:, k % 4, :], ACT.Copy).then_inc(g_high.sem, 1)

            setup()
            act.wait_ge(set_act.sem, 2)
            front_hT(0)
            for j in range(4):
                front_qk(0, j)
            front_norm(0)
            setup_late()
            features(0, 0, range(TILES))
            features(0, 1, range(TILES))

            def after_attend(n, front_next):
                if front_next:
                    front_qk(n + 1, 0)
                    front_qk(n + 1, 1)
                y_copy(n)
                if front_next:
                    front_qk(n + 1, 2)
                    front_qk(n + 1, 3)
                    front_norm(n + 1)
                ffn(n, front_next)

            with act.Fori(0, NB - 1) as i:
                attend(i, True)
                after_attend(i, True)
            attend(NB - 1, False)
            after_attend(NB - 1, False)

        @block.vector
        def _(dve):
            def chain(signal):
                count = [0]

                def step(ins):
                    count[0] += 1
                    ins.then_inc(signal.sem, 1)
                    dve.wait_ge(signal.sem, count[0])
                return step

            def setup_constants():
                for tile, value in ((neg_half[:], -0.5), (state[:], 0.0),
                                    (v_ones[:, :, :, DH:VA], 1.0)):
                    dve.memset(tile, value).then_inc(set_const.sem, 1)
                dve.memset(omega_x[:].bitcast(F32), 0.0).then_inc(om_parts.sem, 1)

            def setup_silu():
                step = chain(set_silu)
                c_col, s_col = (ap[:].rearrange("p k b -> p (k b)") for ap in (cT, sT))
                dve.wait_ge(set_act.sem, 1)
                step(dve.tensor_scalar(ex[:, 0, 0:KT * B], s_col, 1.0, None, ALU.add))
                step(dve.reciprocal(exo[:, 0, 0:KT * B], ex[:, 0, 0:KT * B]))
                step(dve.tensor_tensor(s_col, c_col, exo[:, 0, 0:KT * B], ALU.mult))
                step(dve.tensor_copy(s_rep.rearrange("p k b m -> p (k b) m"),
                                     last_bc(sT[:].rearrange("p k (b o) -> p (k b) o", o=1), P)))

            mod_step = chain(set_mod)

            def setup_mods(step):
                dve.wait_ge(mods_ps.sem, step + 1)
                mods = pa[0][:, 0:8 * B].rearrange("p (m b) -> p b m", b=B)[:, :, 4 * step:4 * step + 4]
                dst = (mod1, mod2)[step][:, :, (0, 2 * C)[step]:]
                mod_step(dve.tensor_scalar(dst[:, :, 0:KT], mods[:, :, 0:KT], 1.0, None, ALU.add))
                mod_step(dve.tensor_copy(dst[:, :, KT:2 * KT], mods[:, :, KT:2 * KT]))
                if step == 0:
                    dve.tensor_copy(mod1_now[:], mod1[:, 0, :]).then_inc(mod1_set.sem, 1)

            def setup_attention():
                dve.wait_ge(ld_attn.sem, 16 * ATTN_LOADS)
                dve.tensor_copy(om_r[:], om_f).then_inc(om_parts.sem, 1)
                dve.tensor_copy(nrow_r[:], nrow_f).then_inc(om_parts.sem, 1)
                qk, v = slice(0, 2 * C), slice(2 * C, 3 * C)
                for k in range(KT):
                    dve.tensor_scalar(wa_r[:, k, qk], wa_raw[k][:, qk], Q_SCALE, None, ALU.mult).then_inc(set_wa.sem, 1)
                    dve.tensor_copy(wa_r[:, k, v], wa_raw[k][:, v]).then_inc(set_wa.sem, 1)
                setup_mods(0)
                dve.wait_ge(om_parts.sem, 2)
                dve.tensor_tensor(om_l[:], om_f, om_r[:].bitcast(F32), ALU.subtract).then_inc(om_parts.sem, 1)
                dve.wait_ge(set_wa.sem, 2 * KT)
                for k in range(KT):
                    dve.scalar_tensor_tensor(wa_l[:, k, qk], wa_raw[k][:, qk], Q_SCALE, wa_r[:, k, qk].bitcast(F32),
                                             ALU.mult, ALU.subtract).then_inc(set_wa.sem, 1)
                    dve.tensor_tensor(wa_l[:, k, v], wa_raw[k][:, v], wa_r[:, k, v].bitcast(F32),
                                      ALU.subtract).then_inc(set_wa.sem, 1)

            def setup_gates():
                for q, dst in enumerate((ga_rows, mod2[:, :, 0:C])):
                    step = chain(set_gate[q])
                    raw = pb[q].rearrange("p (b c) -> p b c", b=B)
                    half_sign, twice_abs = gate_tmp
                    dve.wait_ge(gates_ps.sem, q + 1)
                    step(dve.tensor_scalar(half_sign, raw, 0.0, 0.5, ALU.is_ge, ALU.subtract))
                    step(dve.scalar_tensor_tensor(twice_abs, raw, 4.0, half_sign, ALU.mult, ALU.mult))
                    step(dve.scalar_tensor_tensor(dst, twice_abs, 0.5, half_sign, ALU.max, ALU.mult))

            def row_of(mod, n):
                row = n // BLOCKS_PER_ROW
                return mod[:, row, :] if isinstance(n, int) else \
                    mod[:, bass.ds(row, 1), :].rearrange("p o c -> p (o c)")

            def aggregate(n, vec):
                for t in range(NT):
                    dve.bn_aggr(mv[:, t, :], stats[:, t, :]).then_inc(vec.sem, 1)
                wait(dve, vec, n, 2 * NT)
                dve.tensor_scalar(var_eps[:], mv[:, :, 1], EPS_LN, None, ALU.add).then_inc(vec.sem, 1)
                dve.tensor_scalar(neg_mean[:], mv[:, :, 0], -1.0, None, ALU.mult).then_inc(vec.sem, 1)

            def normalize_apply(n, src, pool, ready):
                wait(dve, pool, n, 1)
                for t in range(NT if src is tok else 2):
                    dve.tensor_scalar(tok[:, t, :], src[:, t, :], mv[:, t, 0:1], rstd[:, t:t + 1],
                                      ALU.subtract, ALU.mult).then_inc(ready.sem, 1)

            def ln1_stats(n, first):
                if first:
                    dve.wait_ge(ld_x.sem, 16)
                else:
                    wait(dve, x_loaded, n - 1, 16)
                for t in range(NT):
                    dve.bn_stats(stats[:, t, :], tok[:, t, :]).then_inc(ln1_vec.sem, 1)
                wait(dve, ln1_vec, n, NT)
                if not first:
                    dve.tensor_copy(mod1_now[:], row_of(mod1, n)).then_inc(mod1_set.sem, 1)
                aggregate(n, ln1_vec)

            def h2_copy(n):
                wait(dve, h2_ps, n, 2)
                dve.tensor_scalar(h_f[:, 1, :], ring[1][:], mod2_cols[:, 1:2], mod2_cols[:, KT + 1:KT + 2],
                                  ALU.mult, ALU.add).then_inc(h2_full[1].sem, 1)

            def split_h(n, rounded, per, parts, ks=range(KT)):
                for k in ks:
                    wait(dve, rounded, n, per * (k + 1))
                    dve.tensor_tensor(h_l[:, k, :], h_f[:, k, :], h_r[:, k, :].bitcast(F32),
                                      ALU.subtract).then_inc(parts.sem, 1)

            def split_qk(n, j):
                wait(dve, sq_ready, n, j + 1)
                dve.scalar_tensor_tensor(qk_l[:, j, :], qk_bank[j][:], qk_bias[:, j:j + 1],
                                         qk_r[:, j, :].bitcast(F32), ALU.add, ALU.subtract).then_inc(qk_split.sem, 1)

            def split_norm(n):
                wait(dve, norm_full, n, 1)
                dve.tensor_tensor(norm_l[:], ring[0][:], norm_r[:].bitcast(F32),
                                  ALU.subtract).then_inc(norm_split.sem, 1)

            def values(n, halves=range(2)):
                for b in halves:
                    wait(dve, v_ps, n, b + 1)
                    dve.tensor_tensor(v_ones[:, 2 * b:2 * b + 2, :, 0:DH],
                                      pb[b].rearrange("p (t h d) -> p t h d", t=2, d=DH),
                                      over_tiles(v_bias[:], 2).rearrange("p t (h d) -> p t h d", d=DH),
                                      ALU.add).then_inc(v_done.sem, 1)

            def setup_late():
                for q in range(4):
                    dve.wait_ge(late_act.sem, q + 1)
                    w = slice(q % 2 * T, (q % 2 + 1) * T)
                    dve.tensor_tensor(wi_l[:, q // 2, w], ring[q][:], wi_r[:, q // 2, w].bitcast(F32),
                                      ALU.subtract).then_inc(late_vec.sem, 1)
                for q in range(4):
                    dve.wait_ge(late_act.sem, 5 + q)
                    two = slice(2 * q, 2 * q + 2)
                    dve.tensor_tensor(wo_l[:, two, :].rearrange("p t c -> p (t c)"), (*pa, *pb)[q][:],
                                      wo_r[:, two, :].rearrange("p t c -> p (t c)").bitcast(F32),
                                      ALU.subtract).then_inc(late_vec.sem, 1)
                for half in range(2):
                    dve.wait_ge(late_act.sem, 10 + half)
                    w = slice(half * T, (half + 1) * T)
                    dve.tensor_tensor(lora_w[32:64, w], ring[1 + half][32:64, :], lora_w[32:64, w].bitcast(F32),
                                      ALU.subtract).then_inc(late_vec.sem, 1)

            def gate_projection():
                dve.wait_ge(ld_late.sem, 16 * LATE_LOADS)
                for row in range(B):
                    dve.tensor_tensor(wp_ga[:, row], wp, over_tiles(ga_rows[:, row], KT),
                                      ALU.mult).then_inc(wp_done.sem, 1)

            def causal_scores(n, q, a):
                wait(dve, a_ps, n, 2 * q + a + 1)
                dve.tensor_tensor(am[:, 2 * (q % 2) + a, :].rearrange("p (c t) -> p c t", c=NT),
                                  score_bank(q, a)[:].rearrange("p (c t) -> p c t", c=NT),
                                  over_tiles(causal, NT), ALU.min).then_inc(am_done.sem, 1)

            def advance_state(n, gr):
                fresh = (n % BLOCKS_PER_ROW + BLOCKS_PER_ROW - 1) // BLOCKS_PER_ROW
                start = state[:, fresh, gr, :] if isinstance(n, int) else \
                    state[:, bass.ds(fresh, 1), gr, :].rearrange("p o m -> p (o m)")
                c0 = (NT + 1) * gr
                wait(dve, d_ps, n, gr + 1)
                dve.tensor_copy(s_sb[:, 0, :], start).then_inc(s_step.sem, 1)
                for c in range(NT):
                    wait(dve, s_step, n, c0 + c + 1)
                    after = s_sb[:, c + 1, :] if c + 1 < NT else state[:, 1, gr, :]
                    dve.tensor_tensor(after, s_sb[:, c, :], prod[:, c, 1, :], ALU.add).then_inc(s_step.sem, 1)

            def add_reads(n, gr):
                wait(dve, read_ps, n, gr + 1)
                dve.tensor_tensor(oT_sb[:], prod_sb[:, :, 0, :], prod[:, :, 1, :], ALU.add).then_inc(oT_added.sem, 1)

            def divide(n, gr):
                wait(dve, o_ps, n, gr + 1)
                if gr == 0:
                    wait(dve, out_done, n, out_done.per)
                o = prod[:, :, 0, :].rearrange("p c (j d) -> p c j d", j=GROUP)
                dve.tensor_scalar(den[:], o[:, :, :, DH], EPS_DEN, None, ALU.add).then_inc(y_step.sem, 1)
                wait(dve, y_step, n, 3 * gr + 1)
                dve.reciprocal(rden[:], den[:]).then_inc(y_step.sem, 1)
                wait(dve, y_step, n, 3 * gr + 2)
                dve.tensor_tensor(y[:, :, gr * GROUP * DH:(gr + 1) * GROUP * DH]
                                  .rearrange("p c (j d) -> p c j d", j=GROUP), o[:, :, :, 0:DH],
                                  rden[:].rearrange("p c (j o) -> p c j o", o=1).broadcast_to([P, NT, GROUP, DH]),
                                  ALU.mult).then_inc(y_step.sem, 1)

            def attend(n, front_next):
                for q in range(2):
                    for a in range(2):
                        causal_scores(n, q, a)
                for gr in range(GROUPS):
                    more = gr + 1 < GROUPS
                    q = 2 * gr + 2
                    wait(dve, prod_ps, n, gr + 1)
                    dve.tensor_copy(prod_sb[:, 2:4].rearrange("p c k m -> p (c k m)"), pb[1])\
                        .then_inc(copied[1].sem, 1)
                    if front_next and gr == GROUPS - 1:
                        split_h(n + 1, hT_r, 2, hT_parts, [1])
                    if more:
                        causal_scores(n, q, 0)
                    advance_state(n, gr)
                    if more:
                        causal_scores(n, q, 1)
                        causal_scores(n, q + 1, 0)
                    elif front_next:
                        split_qk(n + 1, 0)
                    add_reads(n, gr)
                    if gr == GROUPS - 2:
                        causal_scores(n, q + 1, 1)
                    divide(n, gr)
                    if gr < GROUPS - 2:
                        causal_scores(n, q + 1, 1)
                    if front_next and gr == 0:
                        ln1_stats(n + 1, False)
                    if front_next and gr == 1:
                        normalize_apply(n + 1, tok, ln1_pool, hn_ready)
                    if front_next and gr == 2:
                        split_h(n + 1, hT_r, 2, hT_parts, [0])

            def residual(n):
                wait(dve, xr_biased, n, 1)
                for b in range(2):
                    wait(dve, prj_ps, n, b + 1)
                    two = xr[:, 2 * b:2 * b + 2, :].rearrange("p t c -> p (t c)")
                    dve.tensor_tensor(two, pa[b][:], two, ALU.add).then_inc(x2_step.sem, 1)
                    wait(dve, x2_step, n, b + 1)
                    for t in (2 * b, 2 * b + 1):
                        dve.bn_stats(stats[:, t, :], xr[:, t, :]).then_inc(ln2_vec.sem, 1)
                wait(dve, ln2_vec, n, NT)
                dve.tensor_copy(mod2_cols[:], row_of(mod2, n)[:, 2 * C:]).then_inc(mod2c_set.sem, 1)
                aggregate(n, ln2_vec)

            def router(n):
                count = [0]

                def link(ins):
                    count[0] += 1
                    ins.then_inc(rt.sem, 1)

                def after(c=None):
                    wait(dve, rt, n, c or count[0])

                wait(dve, lt_ps, n, 1)
                logit, eq, pr, one1, rest, one2, diff = (route[:, k] for k in range(7))
                m1, m2, pm = rmax[:, 0], rmax[:, 1], rmax[:, 2]
                col = lambda ap: last_bc(ap.rearrange("p (t o) -> p t o", o=1), E)
                link(dve.tensor_tensor(logit, pa[0][:, 0:NT * E].rearrange("p (t e) -> p t e", e=E),
                                       over_tiles(bg_row[:], NT), ALU.add))
                after()

                def first_of_largest(values, largest, one):
                    link(dve.tensor_tensor(eq, values, col(largest), ALU.is_equal))
                    after()
                    link(dve.tensor_tensor(pr, eq, over_tiles(prio, NT), ALU.mult))
                    after()
                    link(dve.tensor_reduce(pm, pr, AX.X, ALU.max))
                    after()
                    link(dve.tensor_tensor(one, pr, col(pm), ALU.is_equal))
                    after()

                link(dve.tensor_reduce(m1, logit, AX.X, ALU.max))
                after()
                first_of_largest(logit, m1, one1)
                link(dve.scalar_tensor_tensor(rest, one1, PAD, logit, ALU.mult, ALU.add))
                after()
                link(dve.tensor_reduce(m2, rest, AX.X, ALU.max))
                after()
                link(dve.tensor_tensor(ex[:, :, 0:E], logit, col(m1), ALU.subtract))
                link(dve.tensor_tensor(ex[:, :, E], m2, m1, ALU.subtract))
                assert count[0] == 10
                first_of_largest(rest, m2, one2)
                link(dve.tensor_tensor(diff, one2, one1, ALU.subtract))
                after()
                for mk, one in ((mk1, one1), (mk2, diff)):
                    for q in range(3):
                        link(dve.tensor_copy(mk[:, :, 32 * q:32 * q + LORA].rearrange("p t (e r) -> p t e r", r=R),
                                             one.rearrange("p t (e o) -> p t e o", o=1)
                                             .broadcast_to([P, NT, E, R])))
                wait(dve, rt_exp, n, 1)
                dve.tensor_copy(r2[:, 0, :].rearrange("p (t m) -> p t m", t=NT), last_bc(exo[:, :, E:E + 1], P))\
                   .then_inc(rt.sem, 1)
                dve.tensor_reduce(wsum[:], exo[:, :, 0:E], AX.X, ALU.add).then_inc(rt.sem, 1)
                return count

            def mask_low(n, front_next):
                if front_next:
                    wait(dve, norm_out, n + 1, 32)
                wait(dve, low_split, n, 1)
                for q, (dst, src) in enumerate(((low1, pa[1][:]), (low2, pa[0][:]))):
                    wait(dve, mask_ps, n, q + 1)
                    dve.tensor_tensor(dst, low.bitcast(F32), src[0:LROWS],
                                      ALU.mult).then_inc(low_masked.sem, 1)

            def experts(n):
                wait(dve, rho_done, n, 1)
                for f in range(FT + 1):
                    if f < FT:
                        wait(dve, z2_ps, n, f + 1)
                        dve.scalar_tensor_tensor(r2[:, f % 2, :], z_bank[f % 4][:], 0.0, rho, ALU.max,
                                                 ALU.mult).then_inc(r2_done.sem, 1)
                    if f >= 1:
                        k = f - 1
                        wait(dve, g_high, n, k + 1)
                        dve.tensor_tensor(g_l[:, k % 3, :], g[:, k % 4, :], g_r[:, k % 3, :].bitcast(F32),
                                          ALU.subtract).then_inc(g_low.sem, 1)
                    if f < FT:
                        wait(dve, r2_done, n, f + 1)
                        dve.tensor_tensor(g[:, f % 4, :], g[:, f % 4, :], r2[:, f % 2, :],
                                          ALU.add).then_inc(g_sum.sem, 1)

            def finish(n):
                wait(dve, wo_mm, n, FT)
                for t in range(NT):
                    dve.scalar_tensor_tensor(tg[:, t // 2, t % 2 * C:(t % 2 + 1) * C],
                                             pa[t // 2][:, t % 2 * C:(t % 2 + 1) * C], w1[:, t:t + 1], gb_now,
                                             ALU.mult, ALU.mult).then_inc(scaled.sem, 1)
                for b in range(2):
                    wait(dve, scaled, n + 1, 2 * b + 2)
                    dve.tensor_tensor(tg[:, b, :], tg[:, b, :],
                                      xr[:, 2 * b:2 * b + 2, :].rearrange("p t c -> p (t c)"),
                                      ALU.add).then_inc(fin.sem, 1)

            def ffn_rest(n, front_next):
                wait(dve, lg_done, n, 1)
                wait(dve, low_high, n, 1)
                dve.tensor_tensor(low[64:96, :], lg[64:96], low[64:96, :].bitcast(F32),
                                  ALU.subtract).then_inc(low_split.sem, 1)
                router(n)
                mask_low(n, front_next)
                wait(dve, rt, n, 23)
                dve.reciprocal(w1[:], wsum[:]).then_inc(rt.sem, 1)
                experts(n)
                finish(n)

            setup_constants()
            ln1_stats(0, True)
            setup_silu()
            normalize_apply(0, tok, ln1_pool, hn_ready)
            setup_attention()
            split_h(0, hT_r, 2, hT_parts)
            for j in range(4):
                split_qk(0, j)
            split_norm(0)
            values(0)
            setup_mods(1)
            setup_gates()
            setup_late()
            gate_projection()

            def after_attend(n, front_next):
                if front_next:
                    split_qk(n + 1, 1)
                    split_qk(n + 1, 2)
                residual(n)
                if front_next:
                    split_qk(n + 1, 3)
                normalize_apply(n, xr, ln2_pool, h2n_ready[0])
                if front_next:
                    split_norm(n + 1)
                h2_copy(n)
                if front_next:
                    values(n + 1, [0])
                split_h(n, h2_r, 1, h2_parts)
                if front_next:
                    values(n + 1, [1])
                ffn_rest(n, front_next)

            with dve.Fori(0, NB - 1) as i:
                attend(i, True)
                after_attend(i, True)
            attend(NB - 1, False)
            after_attend(NB - 1, False)

        @block.gpsimd
        def _(pool):
            def setup():
                pool.memset(low_raw, 0.0).then_inc(set_pool.sem, 1)
                pool.memset(mk1[:], 0.0).then_inc(set_pool.sem, 1)
                pool.memset(mk2[:], 0.0).then_inc(set_pool.sem, 1)
                pool.wait_ge(ld_late.sem, 16 * LATE_LOADS)
                pool.wait_ge(set_pool.sem, 3)
                for half, mk in enumerate((mk1, mk2)):
                    for q in range(3):
                        pool.tensor_copy(mk[:, :, 32 * q:32 * q + LORA],
                                         lora_raw[:, 4 * half:4 * half + 4].rearrange("p t e r -> p t (e r)"))\
                            .then_inc(set_pool.sem, 1)

            def gate_bias():
                pool.wait_ge(set_gate[0].sem, 3)
                pool.tensor_tensor(mod2[:, :, C:2 * C], ga_rows, over_tiles(bp_row, B), ALU.mult)\
                    .then_inc(bias_gated.sem, 1)
                pool.wait_ge(bias_gated.sem, 1)
                pool.wait_ge(set_gate[1].sem, 3)
                pool.wait_ge(set_mod.sem, 4)

            def rstd_of(n, vec, sem):
                wait(pool, vec, n, 2 * NT + 1)
                pool.tensor_tensor(rstd[:], var_eps[:], neg_half[:], ALU.pow).then_inc(sem.sem, 1)
                wait(pool, vec, n, 2 * NT + 2)
                wait(pool, sem, n, 1)
                pool.tensor_tensor(shift[:], neg_mean[:], rstd[:], ALU.mult).then_inc(sem.sem, 1)

            def attend(n, front_next):
                row = n // BLOCKS_PER_ROW
                src = mod2[:, row, 0:2 * C] if isinstance(n, int) else \
                    mod2[:, bass.ds(row, 1), 0:2 * C].rearrange("p o c -> p (o c)")
                pool.tensor_copy(mod2_now[:], src).then_inc(mod2_set.sem, 1)
                if front_next:
                    rstd_of(n + 1, ln1_vec, ln1_pool)

            def residual(n):
                wait(pool, xr_loaded, n, 16)
                wait(pool, mod2_set, n, 1)
                two = xr[:]
                pool.tensor_tensor(two, two, over_tiles(bpg_now, NT), ALU.add).then_inc(xr_biased.sem, 1)

            pool.wait_ge(set_const.sem, 1)
            rstd_of(0, ln1_vec, ln1_pool)
            setup()
            gate_bias()
            with pool.Fori(0, NB - 1) as i:
                attend(i, True)
                residual(i)
                rstd_of(i, ln2_vec, ln2_pool)
                wait(pool, scaled, i + 1, NT)
            attend(NB - 1, False)
            residual(NB - 1)
            rstd_of(NB - 1, ln2_vec, ln2_pool)


def constants():
    import numpy as np
    r = np.arange(P)
    ident = np.eye(P, dtype=np.float32)
    causal = np.where(r[:, None] <= r[None, :], np.finfo(np.float32).max, 0).astype(np.float32)
    headsum = np.zeros((P, VA), np.float32)
    for p in range(P):
        h = p // DH
        headsum[p, h % 2 * GROUP + h // 2] = 1
    prio = np.broadcast_to(np.arange(E, 0, -1, dtype=np.float32), (P, E))
    consts = np.concatenate([ident, causal, headsum, prio], 1)
    rows = np.zeros((4, 2 * M), np.float32)
    for part in range(2):
        for a in range(2):
            rows[2 * part + a, a * M:(a + 1) * M] = -0.5
    return {"consts": np.ascontiguousarray(consts), "norm_rows": rows}


_INS = ['L0_attn_x', 'L0_attn_W_attn', 'L0_attn_b_attn', 'L0_attn_W_proj', 'L0_attn_b_proj', 'L0_attn_omega',
        'L0_ffn_Wg', 'L0_ffn_bg', 'L0_ffn_Wi', 'L0_ffn_Wo', 'L0_ffn_A', 'L0_ffn_B', 'L0_c', 'L0_wmod',
        'consts', 'norm_rows']


def kernel(**inputs):
    import numpy as np
    import concourse.bacc as bacc
    from concourse.bass_utils import run_bass_kernel_spmd

    nc = bacc.Bacc("TRN2", target_bir_lowering=False, num_devices=1)
    inputs = {**inputs, **constants()}
    arrays, args = {}, []
    for name in _INS:
        a = np.ascontiguousarray(inputs[name])
        arrays[f"in_{name}"] = a
        args.append(nc.dram_tensor(f"in_{name}", a.shape, mybir.dt.from_np(a.dtype), kind="ExternalInput").ap())
    out = nc.dram_tensor("out_x", (B, SEQ, C), F32, kind="ExternalOutput").ap()
    parts_out = nc.dram_tensor("qk_parts", (2, 4, P, T), F32, kind="Internal").ap()
    norms_out = nc.dram_tensor("norm_parts", (2, P, T), F32, kind="Internal").ap()
    build(nc, *args, out, parts_out, norms_out)
    r = run_bass_kernel_spmd(nc, [arrays], core_ids=[0])
    return r.results[0]["out_x"]
```
